# Optimizing a Trainium2 kernel written in Bass

```python
import numpy as np
import jax
import jax.numpy as jnp

def _softmax(x, axis=-1):
    return jax.nn.softmax(x, axis=axis)

def _gelu(x):
    return jax.nn.gelu(x, approximate=True)

def _silu(x):
    return jax.nn.silu(x)

def _sigmoid(x):
    return jax.nn.sigmoid(x)

def _layernorm(x, axis=-1, eps=1e-05):
    m = jnp.mean(x, axis=axis, keepdims=True)
    v = jnp.var(x, axis=axis, keepdims=True)
    return (x - m) / jnp.sqrt(v + eps)

def _scatter_add(tgt, idx, src, axis=0):
    return tgt.at[idx].add(src)

def _segment_sum(src, seg, n):
    return jax.ops.segment_sum(src, seg, n)
kernel_name = 'mk_seq_preln_d1_jaxref_r8_27d99e'

def setup_inputs(seed: int=0):
    np.random.seed(seed)
    _w = jnp.asarray

    def _L0_attn_setup():
        import jax, jax.numpy as jnp
        import numpy as np
        HIDDEN = 128
        HEADS = 16
        HEAD = HIDDEN // HEADS

        def _ternary_weight(key, shape):
            g = jax.random.normal(key, shape, dtype=jnp.float32)
            return jnp.where(jnp.abs(g) < 0.6, 0.0, jnp.sign(g)).astype(jnp.float32)

        def _tlin(x, w, s, b):
            return jnp.einsum('bsh,oh->bso', x, w) * s + b
        key = jax.random.key(seed)
        ks = jax.random.split(key, 10)
        x = jax.random.normal(ks[0], (2, 256, HIDDEN), dtype=jnp.float32)
        d = {'x': x}
        names = ['q', 'k', 'v', 'o']
        for i, n in enumerate(names):
            d[f'w_{n}'] = _ternary_weight(ks[1 + i], (HIDDEN, HIDDEN))
            d[f's_{n}'] = jnp.float32(0.02)
            d[f'b_{n}'] = jax.random.normal(ks[5 + i], (HIDDEN,), dtype=jnp.float32) * 0.02
        return d
    _L0_attn_in = _L0_attn_setup()

    def _L0_ffn_setup():
        import jax, jax.numpy as jnp
        import numpy as np
        NUM_TRUE = 8
        NUM_NULL = 2
        NUM_EXPERTS = NUM_TRUE + NUM_NULL
        TOP_K = 2
        key = jax.random.key(seed)
        k0, k1, k2 = jax.random.split(key, 3)
        B, S, D = (4, 256, 128)
        inputs = jax.random.normal(k0, (B, S, D), dtype=jnp.float32)
        gate_w = jax.random.normal(k1, (NUM_EXPERTS, D), dtype=jnp.float32) * 0.02
        gate_b = jnp.zeros((NUM_EXPERTS,), dtype=jnp.float32)
        expert_w = jax.random.normal(k2, (NUM_TRUE, D, D), dtype=jnp.float32) * 0.02
        expert_b = jnp.zeros((NUM_TRUE, D), dtype=jnp.float32)
        return {'inputs': inputs, 'gate_w': gate_w, 'gate_b': gate_b, 'expert_w': expert_w, 'expert_b': expert_b}
    _L0_ffn_in = _L0_ffn_setup()
    _d = {'L0_attn_x': _L0_attn_in['x'], 'L0_attn_w_q': _L0_attn_in['w_q'], 'L0_attn_s_q': _L0_attn_in['s_q'], 'L0_attn_b_q': _L0_attn_in['b_q'], 'L0_attn_w_k': _L0_attn_in['w_k'], 'L0_attn_s_k': _L0_attn_in['s_k'], 'L0_attn_b_k': _L0_attn_in['b_k'], 'L0_attn_w_v': _L0_attn_in['w_v'], 'L0_attn_s_v': _L0_attn_in['s_v'], 'L0_attn_b_v': _L0_attn_in['b_v'], 'L0_attn_w_o': _L0_attn_in['w_o'], 'L0_attn_s_o': _L0_attn_in['s_o'], 'L0_attn_b_o': _L0_attn_in['b_o'], 'L0_ffn_gate_w': _L0_ffn_in['gate_w'], 'L0_ffn_gate_b': _L0_ffn_in['gate_b'], 'L0_ffn_expert_w': _L0_ffn_in['expert_w'], 'L0_ffn_expert_b': _L0_ffn_in['expert_b']}
    _x0 = _d['L0_attn_x']
    _d['L0_attn_x'] = jax.random.normal(jax.random.fold_in(jax.random.key(seed), 1), (8, 512, 128), dtype=_x0.dtype)
    del _x0
    return _d

def reference(L0_attn_x, L0_attn_w_q, L0_attn_s_q, L0_attn_b_q, L0_attn_w_k, L0_attn_s_k, L0_attn_b_k, L0_attn_w_v, L0_attn_s_v, L0_attn_b_v, L0_attn_w_o, L0_attn_s_o, L0_attn_b_o, L0_ffn_gate_w, L0_ffn_gate_b, L0_ffn_expert_w, L0_ffn_expert_b):

    def _L0_attn_ref(x, w_q, s_q, b_q, w_k, s_k, b_k, w_v, s_v, b_v, w_o, s_o, b_o):
        import jax, jax.numpy as jnp
        import numpy as np
        HIDDEN = 128
        HEADS = 16
        HEAD = HIDDEN // HEADS

        def _ternary_weight(key, shape):
            g = jax.random.normal(key, shape, dtype=jnp.float32)
            return jnp.where(jnp.abs(g) < 0.6, 0.0, jnp.sign(g)).astype(jnp.float32)

        def _tlin(x, w, s, b):
            return jnp.einsum('bsh,oh->bso', x, w) * s + b
        B, S, H = x.shape

        def split_heads(t):
            return t.reshape(B, S, HEADS, HEAD).transpose(0, 2, 1, 3)
        q = split_heads(_tlin(x, w_q, s_q, b_q))
        k = split_heads(_tlin(x, w_k, s_k, b_k))
        v = split_heads(_tlin(x, w_v, s_v, b_v))
        scores = jnp.einsum('bhqd,bhkd->bhqk', q, k) / jnp.sqrt(jnp.float32(HEAD))
        attn = jax.nn.softmax(scores, axis=-1)
        ctx = jnp.einsum('bhqk,bhkd->bhqd', attn, v)
        ctx = ctx.transpose(0, 2, 1, 3).reshape(B, S, H)
        return _tlin(ctx, w_o, s_o, b_o)

    def _L0_ffn_ref(inputs, gate_w, gate_b, expert_w, expert_b):
        import jax, jax.numpy as jnp
        import numpy as np
        NUM_TRUE = 8
        NUM_NULL = 2
        NUM_EXPERTS = NUM_TRUE + NUM_NULL
        TOP_K = 2
        D = inputs.shape[-1]
        x = inputs.reshape(-1, D)
        gate_logits = x @ gate_w.T + gate_b
        gate_probs = jax.nn.softmax(gate_logits, axis=-1)
        weights, selected = jax.lax.top_k(gate_probs, TOP_K)
        true_mask = selected < NUM_TRUE
        true_weights = weights * true_mask
        denom = true_weights.sum(axis=-1, keepdims=True)
        denom = jnp.where(denom > 0, denom, jnp.ones_like(denom))
        norm_w = (true_weights / denom).astype(x.dtype)
        one_hot = jax.nn.one_hot(selected, NUM_EXPERTS, dtype=norm_w.dtype)
        combine_w = jnp.einsum('tk,tke->te', norm_w, one_hot)[:, :NUM_TRUE]
        expert_out = jnp.einsum('td,edh->teh', x, expert_w) + expert_b[None, :, :]
        out = jnp.einsum('te,teh->th', combine_w, expert_out)
        return out.reshape(inputs.shape[:-1] + (out.shape[-1],))
    x = L0_attn_x
    x = x + _L0_attn_ref(_layernorm(x, axis=-1), L0_attn_w_q, L0_attn_s_q, L0_attn_b_q, L0_attn_w_k, L0_attn_s_k, L0_attn_b_k, L0_attn_w_v, L0_attn_s_v, L0_attn_b_v, L0_attn_w_o, L0_attn_s_o, L0_attn_b_o)
    x = x + _L0_ffn_ref(_layernorm(x, axis=-1), L0_ffn_gate_w, L0_ffn_gate_b, L0_ffn_expert_w, L0_ffn_expert_b)
    return x

_drawn_inputs = setup_inputs


def setup_inputs(seed=0):
    import zlib

    import numpy as np

    out = dict(_drawn_inputs(seed))
    spreads = {'L0_ffn_gate_b': (0.0, 0.1), 'L0_ffn_expert_b': (0.0, 0.1)}
    factors = {'L0_attn_w_q': 8.0,
     'L0_attn_b_q': 8.0,
     'L0_attn_w_k': 8.0,
     'L0_attn_b_k': 8.0,
     'L0_attn_w_v': 7.414,
     'L0_attn_b_v': 8.0,
     'L0_attn_w_o': 6.257}
    for name, (base, spread) in spreads.items():
        noise = np.random.default_rng([zlib.crc32(name.encode()), seed]).standard_normal(out[name].shape)
        drawn = base * np.exp(spread * noise) if base else spread * noise
        out[name] = jnp.asarray(drawn.astype(out[name].dtype))
    for name, factor in factors.items():
        out[name] = (out[name] * factor).astype(out[name].dtype)
    return out
```

```python
from contextlib import ExitStack

import numpy as np

import concourse.bass as bass
from concourse import mybir

F32 = mybir.dt.float32
BF16 = mybir.dt.bfloat16
ALU = mybir.AluOpType
ACT = mybir.ActivationFunctionType
AX_X = mybir.AxisListType.X

P = 128
EPS = 1e-5
HEADS, HD = 16, 8
JP = HEADS // 2
TOPW = 10
NE = 8
ROWS_QK = 6 * HD
ROWS_ST = ROWS_QK + 3
SLOTS = 64
GATE_STEPS = 22
W_DMAS = 5
POOL_SETUP_EB = 10
DVE_SETUP = 2
LOADS = 24

Q_TERMS = (0, 0, 0, 1, 1, 2)
K_TERMS = (0, 1, 2, 0, 1, 0)

TASKS = (
    (5, "rows1", "A"), (7, "xn_t", "F"), (8, "ctx3", "T"), (9, "q", "F"), (11, "k", "F"),
    (13, "ctx_t", "T"), (14, "v", "F"), (16, "proj", "T"), (21, "rows2", "A"), (23, "ctx0", "A"),
    (28, "xn2_t", "T"), (31, "logits", "T"), (37, "rows3", "A"), (39, "ctx1", "A"),
    (43, "e0a", "T"), (45, "e0b", "T"), (47, "e1a", "T"), (49, "e1b", "T"), (51, "e2a", "T"),
    (52, "e2b", "T"), (54, "rows0", "F"), (56, "ctx2", "A"), (58, "e3a", "T"), (60, "e3b", "T"),
)
DESK = {name: n % 2 for n, (_, name, _) in enumerate(TASKS)}
PE_SLOT = {slot: name for slot, name, _ in TASKS}
WHO = {name: who for _, name, who in TASKS}


def head_of(g, c):
    return 2 * g + c // 2, c % 2


W_QK, W_V, W_O, W_GATE, W_END = 0, 2 * P, 3 * P, 4 * P, 4 * P + TOPW
V_BV, V_BO, V_BG, V_SCALES, V_END = 0, 4 * P, 5 * P, 5 * P + TOPW, 5 * P + TOPW + 4


def build(nc, x, weights, experts, vectors, qk_biases, expert_b, out):
    B, S, D = x.shape
    QT = S // P
    assert D == P and S == 512 and HEADS * HD == D and experts.shape[1] == NE * D

    def present(b):
        return {"A": 0 <= b < B, "F": b + 1 < B, "T": b >= 1}

    def uses(b, desk):
        return sum(present(b)[who] for _, name, who in TASKS if DESK[name] == desk)

    def place(b, name, inner):
        desk = DESK[name]
        first = 1 if inner else b
        here = present(first)
        n = sum(uses(bb, desk) for bb in range(-1, first))
        for _, other, who in TASKS:
            if other == name:
                break
            n += here[who] and DESK[other] == desk
        return n + (b - 1) * uses(1, desk) if inner else n

    ctx = ExitStack()
    with ctx:
        def sb(name, shape, dt=F32):
            return ctx.enter_context(nc.sbuf_tensor(name, shape, dt))

        def ps(name):
            return ctx.enter_context(nc.psum_tensor(name, [P, 512], F32))

        def sem(name):
            return ctx.enter_context(nc.semaphore(name))

        st_bank = [ps(f"st_bank{i}") for i in range(2)]
        s_bank = [ps(f"s_bank{i}") for i in range(2)]
        pv_bank = ps("pv_bank")
        desk_bank = [ps(f"desk_bank{i}") for i in range(2)]

        identity = sb("identity", [P, P])
        identity_bf = sb("identity_bf", [P, P], BF16)
        w_all = sb("w_all", [P, W_END])
        w_qk_t = w_all[:, W_QK:W_V].rearrange("i (n o) -> i n o", n=2)
        w_v_t = w_all[:, W_V:W_O]
        w_o_t = w_all[:, W_O:W_GATE]
        gate_t = w_all[:, W_GATE:W_END]
        w_exp = sb("w_exp", [P, NE * P])
        vec_all = sb("vec_all", [P, V_END])
        b_v_all = vec_all[:, V_BV:V_BO]
        b_o_all = vec_all[:, V_BO:V_BG]
        gate_b_all = vec_all[:, V_BG:V_SCALES]
        scales = vec_all[:, V_SCALES:V_END]
        eb_row = sb("eb_row", [1, NE * P])
        eb_rest = sb("eb_rest", [1, NE * P])
        eb_parts = sb("eb_parts", [1, 3, NE * P], BF16)
        eb_rows = sb("eb_rows", [3, NE * P], BF16)
        ones3 = sb("ones3", [3, P], BF16)
        qk_scale = sb("qk_scale", [P, 2])
        qk_bias_nat = sb("qk_bias_nat", [P, 2])
        qk_bias = sb("qk_bias", [P, 2])
        neg_half = sb("neg_half", [P, QT])
        zeros = sb("zeros", [P, QT * 4])
        order = sb("order", [P, QT, TOPW])

        x_all = sb("x_all", [P, B * QT, P])
        stats = sb("stats", [P, QT, 6])
        mean_var = sb("mean_var", [P, QT, 2])
        var_eps = sb("var_eps", [P, QT])
        rstd = sb("rstd", [P, QT])
        x_centred = sb("x_centred", [P, QT, P])
        xn = sb("xn", [P, QT, P])
        xn_t = sb("xn_t", [P, S])
        qk_full = sb("qk_full", [P, 2, S])
        qk_rest = sb("qk_rest", [P, 2, S])
        qk_parts = sb("qk_parts", [P, 2, 3, S], BF16)
        q_rows = [sb(f"q_rows{i}", [P, JP, S], BF16) for i in range(2)]
        k_rows = [sb(f"k_rows{i}", [P, JP, S], BF16) for i in range(2)]
        v_ones = [sb(f"v_ones{i}", [P, QT, HEADS, 32]) for i in range(2)]
        neg_max = sb("neg_max", [P, 2, QT, 4])
        neg_rest = sb("neg_rest", [P, QT * 4])
        max_parts = sb("max_parts", [P, 2, QT, 12], BF16)
        max_rows = sb("max_rows", [12, 2, S], BF16)
        probs = sb("probs", [P, 8, S])
        ctx_raw = sb("ctx_raw", [P, 2, S])
        inv_sum = sb("inv_sum", [P, QT, 4])
        ctx_tok = sb("ctx_tok", [P, QT, P])
        ctx_t = sb("ctx_t", [P, S])
        x_bias = sb("x_bias", [P, QT, P])
        x1 = sb("x1", [P, QT, P])
        stats2 = sb("stats2", [P, QT, 6])
        mean_var2 = sb("mean_var2", [P, QT, 2])
        var_eps2 = sb("var_eps2", [P, QT])
        rstd2 = sb("rstd2", [P, QT])
        x1_centred = sb("x1_centred", [P, QT, P])
        xn2 = sb("xn2", [P, QT, P])
        xn2_t = sb("xn2_t", [P, S])
        logits = sb("logits", [P, QT, TOPW])
        g4 = sb("g4", [P, 10, QT])
        g10 = sb("g10", [P, 10, QT, TOPW])
        true_w = sb("true_w", [P, QT, NE])
        chosen = sb("chosen", [P, QT, NE])
        combine_w = sb("combine_w", [P, QT, NE])
        prod = sb("prod", [P, QT, NE, P])
        sum4 = sb("sum4", [P, 4, P])
        sum2 = sb("sum2", [P, 2, P])
        sum1 = sb("sum1", [P, P])
        y = sb("y", [P, QT, P])

        w_loaded = sem("w_loaded")
        x0_loaded = sem("x0_loaded")
        x_loaded = sem("x_loaded")
        pool_setup = sem("pool_setup")
        dve_setup = sem("dve_setup")
        eb_loaded = sem("eb_loaded")
        filled = [sem("desk0_filled"), sem("desk1_filled")]
        emptied = [sem("desk0_emptied"), sem("desk1_emptied")]
        ln1 = sem("ln1")
        ln1_centred = sem("ln1_centred")
        xn_ready = sem("xn_ready")
        qk_split = sem("qk_split")
        rows_qk = sem("rows_qk")
        s_filled = sem("s_filled")
        max_done = sem("max_done")
        max_split = sem("max_split")
        rows_max = sem("rows_max")
        st_filled = sem("st_filled")
        exp_done = sem("exp_done")
        pv_done = sem("pv_done")
        pv_taken = sem("pv_taken")
        inv_done = sem("inv_done")
        xb_ready = sem("xb_ready")
        x1_ready = sem("x1_ready")
        ln2 = sem("ln2")
        ln2_centred = sem("ln2_centred")
        xn2_ready = sem("xn2_ready")
        gate = sem("gate")
        gate_exp = sem("gate_exp")
        mixed = sem("mixed")
        stored = sem("stored")

        block = ctx.enter_context(nc.Block())

        def wait(eng, semaphore, count):
            if not (isinstance(count, int) and count <= 0):
                eng.wait_ge(semaphore, count)

        def wait_filled(eng, b, name, inner):
            wait(eng, filled[DESK[name]], place(b, name, inner) + 1)

        def wait_emptied(eng, b, name, inner):
            wait(eng, emptied[DESK[name]], place(b, name, inner) + 1)

        def bodies(eng, body):
            body(-1, 1, False)
            body(0, 0, False)
            with eng.Fori(1, B - 2, 2) as b:
                body(b, 1, True)
                body(b + 1, 0, True)
            body(B - 1, 1, False)
            body(B, 0, False)

        def parts_of(b, inner):
            return (True, True, True) if inner else tuple(present(b)[w] for w in "AFT")

        @block.sync
        def _(sync):
            x_v = x.rearrange("b (p t) d -> p b (t d)", p=P)
            out_v = out.rearrange("b (p t) d -> p b (t d)", p=P)
            sync.dma_start(x_all[:, 0:QT, :], x_v[:, 0, :]).then_inc(x0_loaded, 16)
            sync.dma_start(w_all[:, :], weights).then_inc(w_loaded, 16)
            sync.dma_start(vec_all[:, :], vectors.partition_broadcast(P)).then_inc(w_loaded, 16)
            sync.dma_start(qk_bias_nat[:, :], qk_biases).then_inc(w_loaded, 16)
            sync.dma_start(eb_row[:, :], expert_b.rearrange("(a e) h -> a (e h)", a=1)).then_inc(w_loaded, 16)
            sync.dma_start(w_exp[:, :], experts).then_inc(w_loaded, 16)
            for b in range(1, B):
                sync.dma_start(x_all[:, b * QT:(b + 1) * QT, :], x_v[:, b, :]).then_inc(x_loaded, 16)
            sync.wait_ge(pool_setup, POOL_SETUP_EB)
            sync.dma_start(eb_rows[:, :], eb_parts[:, :, :]).then_inc(eb_loaded, 16)

            def put_max_rows(b, g, par, inner):
                name = f"rows{g}"
                wait_emptied(sync, b - (g == 0), name, inner)
                for h in range(2):
                    sync.dma_start(q_rows[par][64 * h + ROWS_QK:64 * h + ROWS_ST, 2 * g:2 * g + 2, :],
                                   max_rows[6 * h:6 * h + 6, g % 2, :]).then_inc(rows_max, 16)

            def body(b, par, inner):
                A, F, T = parts_of(b, inner)
                if A:
                    put_max_rows(b, 1, par, inner)
                if F:
                    wait(sync, st_filled, SLOTS * b)
                    for n, (rows, terms) in enumerate(((q_rows[1 - par], Q_TERMS), (k_rows[1 - par], K_TERMS))):
                        wait(sync, qk_split, 6 * (b + 1) + 3 * n + 3)
                        for t, part in enumerate(terms):
                            for h in range(2):
                                lo = 64 * h + HD * t
                                sync.dma_start(rows[lo:lo + HD, :, :],
                                               qk_parts[64 * h:64 * h + 64, n, part, :]).then_inc(rows_qk, 16)
                if A:
                    put_max_rows(b, 2, par, inner)
                    put_max_rows(b, 3, par, inner)
                if F:
                    put_max_rows(b + 1, 0, 1 - par, inner)
                if T:
                    wait(sync, mixed, 16 * b)
                    sync.dma_start(out_v[:, bass.ds(b - 1, 1), :], y[:, :, :].rearrange("p (a t) d -> p a (t d)", a=1))\
                        .then_inc(stored, 16)

            bodies(sync, body)
            sync.wait_ge(stored, 16 * B)

        @block.gpsimd
        def _(pool):
            pool.memset(identity[:, :], 0.0).then_inc(pool_setup, 1)
            pool.wait_ge(pool_setup, 1)
            pool.affine_select(out=identity[:, :], in_=identity[:, :], compare_op=ALU.not_equal, fill=1.0,
                               base=0, pattern=[[-1, P]], channel_multiplier=1).then_inc(pool_setup, 1)
            pool.wait_ge(pool_setup, 2)
            pool.tensor_copy(identity_bf[:, :], identity[:, :]).then_inc(pool_setup, 1)
            pool.wait_ge(w_loaded, W_DMAS * 16)
            pool.tensor_copy(eb_parts[:, 0, :], eb_row[:, :]).then_inc(pool_setup, 1)
            pool.wait_ge(pool_setup, 4)
            pool.tensor_tensor(eb_parts[:, 1, :], eb_row[:, :], eb_parts[:, 0, :], ALU.subtract)\
                .then_inc(pool_setup, 1)
            pool.tensor_tensor(eb_rest[:, :], eb_row[:, :], eb_parts[:, 0, :], ALU.subtract)\
                .then_inc(pool_setup, 1)
            pool.wait_ge(pool_setup, 6)
            pool.tensor_tensor(eb_parts[:, 2, :], eb_rest[:, :], eb_parts[:, 1, :], ALU.subtract)\
                .then_inc(pool_setup, 1)
            pool.memset(ones3[:, :], 1.0).then_inc(pool_setup, 1)
            for n in range(TOPW):
                last = pool.memset(order[:, :, n:n + 1], float(TOPW - n))
            last.then_inc(pool_setup, 1)
            pool.wait_ge(pool_setup, 9)
            pool.memset(zeros[:, :], 0.0)
            pool.memset(neg_half[:, :], -0.5).then_inc(pool_setup, 1)
            pool.wait_ge(pool_setup, 10)

            def split_max(b, g):
                n = 4 * b + g
                r = g % 2
                whole = neg_max[:, r, :, :]

                def part(k):
                    return max_parts[:, r, :, :].rearrange("p t (h k c) -> p t h k c", h=2, k=3)[:, :, :, k, :]
                w4 = whole.rearrange("p t (h c) -> p t h c", h=2)
                zeros4 = zeros[:, :].rearrange("p (t h c) -> p t h c", h=2, c=2)
                rest = neg_rest[:, :].rearrange("p (t h c) -> p t h c", h=2, c=2)
                wait(pool, max_done, 16 * (n + 1))
                pool.tensor_tensor(part(0), w4, zeros4, ALU.add).then_inc(max_split, 1)
                pool.wait_ge(max_split, 4 * n + 1)
                pool.tensor_tensor(part(1), w4, part(0), ALU.subtract).then_inc(max_split, 1)
                pool.tensor_tensor(rest, w4, part(0), ALU.subtract).then_inc(max_split, 1)
                pool.wait_ge(max_split, 4 * n + 3)
                pool.tensor_tensor(part(2), rest, part(1), ALU.subtract).then_inc(max_split, 1)

            def per_token(v):
                return v.unsqueeze(2).to_broadcast([P, QT, P])

            def mix(b, t):
                n = 16 * (b - 1) + 4 * t
                if t == 0:
                    wait(pool, stored, 16 * (b - 1))
                pool.tensor_tensor(sum4[:, :, :], prod[:, t, 0:4, :], prod[:, t, 4:8, :], ALU.add).then_inc(mixed, 1)
                pool.wait_ge(mixed, n + 1)
                pool.tensor_tensor(sum2[:, :, :], sum4[:, 0:2, :], sum4[:, 2:4, :], ALU.add).then_inc(mixed, 1)
                pool.wait_ge(mixed, n + 2)
                pool.tensor_tensor(sum1[:, :], sum2[:, 0, :], sum2[:, 1, :], ALU.add).then_inc(mixed, 1)
                pool.wait_ge(mixed, n + 3)
                pool.tensor_tensor(y[:, t, :], sum1[:, :], x1[:, t, :], ALU.add).then_inc(mixed, 1)

            def body(b, par, inner):
                A, F, T = parts_of(b, inner)
                if A:
                    split_max(b, 1)
                if F:
                    wait(pool, ln1, 3 * (b + 1) + 2)
                    pool.tensor_tensor(x_centred[:, :, :], x_all[:, bass.ts(b + 1, QT), :],
                                       per_token(mean_var[:, :, 0]), ALU.subtract).then_inc(ln1_centred, 1)
                    wait(pool, ln1, 3 * (b + 1) + 3)
                    pool.tensor_tensor(rstd[:, :], var_eps[:, :], neg_half[:, :], ALU.pow).then_inc(ln1_centred, 1)
                    wait(pool, ln1_centred, 2 * (b + 2))
                    pool.tensor_tensor(xn[:, :, :], x_centred[:, :, :], per_token(rstd[:, :]), ALU.mult)\
                        .then_inc(xn_ready, 1)
                if T:
                    pool.tensor_tensor(x_bias[:, :, :], x_all[:, bass.ts(b - 1, QT), :],
                                       b_o_all.unsqueeze(1).to_broadcast([P, QT, P]), ALU.add)\
                        .then_inc(xb_ready, 1)
                if F:
                    for n, name in enumerate("qk"):
                        c = 6 * (b + 1) + 3 * n
                        wait_emptied(pool, b, name, inner)
                        pool.tensor_tensor(qk_parts[:, n, 1, :], qk_full[:, n, :], qk_parts[:, n, 0, :],
                                           ALU.subtract).then_inc(qk_split, 1)
                        pool.tensor_tensor(qk_rest[:, n, :], qk_full[:, n, :], qk_parts[:, n, 0, :],
                                           ALU.subtract).then_inc(qk_split, 1)
                        pool.wait_ge(qk_split, c + 2)
                        pool.tensor_tensor(qk_parts[:, n, 2, :], qk_rest[:, n, :], qk_parts[:, n, 1, :],
                                           ALU.subtract).then_inc(qk_split, 1)
                if A:
                    split_max(b, 2)
                if T:
                    wait(pool, ln2, 3 * (b - 1) + 2)
                    pool.tensor_tensor(x1_centred[:, :, :], x1[:, :, :],
                                       per_token(mean_var2[:, :, 0]), ALU.subtract).then_inc(ln2_centred, 1)
                    wait(pool, ln2, 3 * (b - 1) + 3)
                    pool.tensor_tensor(rstd2[:, :], var_eps2[:, :], neg_half[:, :], ALU.pow).then_inc(ln2_centred, 1)
                    wait(pool, ln2_centred, 2 * b)
                    pool.tensor_tensor(xn2[:, :, :], x1_centred[:, :, :], per_token(rstd2[:, :]), ALU.mult)\
                        .then_inc(xn2_ready, 1)
                if A:
                    split_max(b, 3)
                for t in range(QT):
                    if T:
                        wait_emptied(pool, b, f"e{t}b", inner)
                        mix(b, t)
                    if F and t == 0:
                        split_max(b + 1, 0)

            pool.wait_ge(x0_loaded, 16)
            pool.wait_ge(x_loaded, 16 * (B - 1))
            bodies(pool, body)

        @block.scalar
        def _(act):
            def take_pv(b, g):
                n = 4 * b + g
                wait(act, pv_done, 4 * n + 4)
                act.copy(ctx_raw[:, g % 2, :], pv_bank[:, :]).then_inc(pv_taken, 1)

            def take_rows(b, name, inner):
                g = int(name[-1])
                wait_filled(act, b, name, inner)
                act.copy(max_rows[:, g % 2, :], desk_bank[DESK[name]][0:12, 0:S // 2].bitcast(BF16))\
                    .then_inc(emptied[DESK[name]], 1)

            def take(b, name, dst, inner):
                wait_filled(act, b, name, inner)
                act.copy(dst[:, :], desk_bank[DESK[name]][:, :]).then_inc(emptied[DESK[name]], 1)

            def body(b, par, inner):
                A, F, T = parts_of(b, inner)
                for s in range(SLOTS):
                    if A:
                        a = SLOTS * b + s
                        wait(act, st_filled, a + 1)
                        if s % 4 == 0:
                            wait(act, pv_done, 16 * b + s // 4 - 1)
                        act.activation(probs[:, s % 8, :], st_bank[s % 2][:, :], ACT.Exp).then_inc(exp_done, 1)
                    if s == 5 and T:
                        take_pv(b - 1, 3)
                    if s == 6 and A:
                        take_rows(b, "rows1", inner)
                    if s == 8 and F:
                        take(b, "xn_t", xn_t, inner)
                    if s in (10, 12) and F:
                        n, name = (0, "q") if s == 10 else (1, "k")
                        bank = desk_bank[DESK[name]]
                        wait_filled(act, b, name, inner)
                        act.activation(qk_parts[:, n, 0, :], bank[:, :], ACT.Identity,
                                       scale=qk_scale[:, n:n + 1], bias=qk_bias[:, n:n + 1])
                        act.activation(qk_full[:, n, :], bank[:, :], ACT.Identity,
                                       scale=qk_scale[:, n:n + 1], bias=qk_bias[:, n:n + 1])\
                            .then_inc(emptied[DESK[name]], 1)
                    if s == 14 and T:
                        take(b, "ctx_t", ctx_t, inner)
                    if s == 21 and A:
                        take_pv(b, 0)
                    if s == 22 and A:
                        take_rows(b, "rows2", inner)
                    if s == 29 and T:
                        take(b, "xn2_t", xn2_t, inner)
                    if s == 35 and T:
                        wait(act, gate, GATE_STEPS * (b - 1) + 2)
                        act.activation(g10[:, 1, :, :], g10[:, 0, :, :], ACT.Exp).then_inc(gate_exp, 1)
                    if s == 37 and A:
                        take_pv(b, 1)
                    if s == 38 and A:
                        take_rows(b, "rows3", inner)
                    if s == 53 and A:
                        take_pv(b, 2)
                    if s == 55 and F:
                        take_rows(b, "rows0", inner)

            act.wait_ge(dve_setup, DVE_SETUP)
            bodies(act, body)

        @block.vector
        def _(dve):
            for i in range(2):
                nc.vector.memset(k_rows[i][32:64, :, :], 1.0)
                nc.vector.memset(k_rows[i][96:128, :, :], 1.0)
                nc.vector.memset(v_ones[i][:, :, :, HD + 1:32], 0.0)
                last = nc.vector.memset(v_ones[i][:, :, :, HD:HD + 1], 1.0)
            last.then_inc(dve_setup, 1)
            dve.wait_ge(w_loaded, W_DMAS * 16)
            root = float(1.0 / np.sqrt(np.float32(HD)))
            nc.vector.tensor_scalar(qk_scale[:, 0:1], scales[:, 0:1], root, None, ALU.mult)
            nc.vector.tensor_copy(qk_scale[:, 1:2], scales[:, 1:2])
            nc.vector.tensor_scalar(qk_bias[:, 0:1], qk_bias_nat[:, 0:1], root, None, ALU.mult)
            nc.vector.tensor_copy(qk_bias[:, 1:2], qk_bias_nat[:, 1:2]).then_inc(dve_setup, 1)
            dve.wait_ge(pool_setup, POOL_SETUP_EB)
            dve.wait_ge(x0_loaded, 16)
            dve.wait_ge(x_loaded, 16 * (B - 1))

            def norm_ctx(b, g, body_b, inner):
                n, name = 4 * b + g, f"ctx{g}"
                wait_filled(dve, body_b, name, inner)
                bank = desk_bank[DESK[name]][:, :].rearrange("p (t c k) -> p t c k", t=QT, k=32)
                nc.vector.reciprocal(inv_sum[:, :, :], bank[:, :, :, HD]).then_inc(inv_done, 1)
                wait(dve, inv_done, n + 1)
                nc.vector.tensor_tensor(
                    ctx_tok[:, :, 32 * g:32 * g + 32].rearrange("p t (c d) -> p t c d", d=HD),
                    bank[:, :, :, 0:HD], inv_sum[:, :, :].unsqueeze(3).to_broadcast([P, QT, 4, HD]),
                    ALU.mult).then_inc(emptied[DESK[name]], 1)

            def weigh(b, t, half, inner):
                name = f"e{t}{'ab'[half]}"
                wait_filled(dve, b, name, inner)
                nc.vector.tensor_tensor(
                    prod[:, t, 4 * half:4 * half + 4, :],
                    desk_bank[DESK[name]][:, :].rearrange("p (e d) -> p e d", e=4),
                    combine_w[:, t, 4 * half:4 * half + 4].unsqueeze(2).to_broadcast([P, 4, P]),
                    ALU.mult).then_inc(emptied[DESK[name]], 1)

            WEIGH = {46: (0, 0), 47: (0, 1), 49: (1, 0), 51: (1, 1), 53: (2, 0), 54: (2, 1), 60: (3, 0), 62: (3, 1)}

            def body(b, par, inner):
                A, F, T = parts_of(b, inner)

                def step(n, instruction):
                    instruction.then_inc(gate, 1)

                def after(n):
                    wait(dve, gate, GATE_STEPS * (b - 1) + n)

                def wide(v):
                    return v.unsqueeze(2).to_broadcast([P, QT, TOPW])

                V = nc.vector
                for s in range(SLOTS):
                    if s == 1 and F:
                        wait(dve, ln1, 3 * (b + 1) + 1)
                    if s == 20 and T:
                        wait(dve, ln2, 3 * (b - 1) + 1)
                    if (A if s < 32 else F):
                        u = SLOTS * b + s + 32
                        g, t, c = (s // 16 + 2) % 4, s % 16 // 4, (s % 4) ^ 1
                        col = 2 * (c % 2) + c // 2
                        wait(dve, s_filled, u + 1)
                        V.reduce_max(neg_max[:, g % 2, t, col:col + 1], s_bank[s % 2][:, :], AX_X,
                                     negate=True).then_inc(max_done, 1)
                    if s == 0 and F:
                        for t in range(QT):
                            last = V.bn_stats(stats[:, t, :], x_all[:, bass.ts((b + 1) * QT + t, 1), :]
                                              .rearrange("p a d -> p (a d)"))
                        last.then_inc(ln1, 1)
                    if s == 1 and F:
                        for t in range(QT):
                            last = V.bn_aggr(mean_var[:, t, :], stats[:, t, :])
                        last.then_inc(ln1, 1)
                    if s == 2 and F:
                        wait(dve, ln1, 3 * (b + 1) + 2)
                        V.tensor_scalar(var_eps[:, :], mean_var[:, :, 1], EPS, None, ALU.add).then_inc(ln1, 1)
                    if s == 10 and T:
                        norm_ctx(b - 1, 3, b, inner)
                    if s == 15 and F:
                        wait_filled(dve, b, "v", inner)
                        V.scalar_tensor_tensor(
                            out=v_ones[1 - par][:, :, :, 0:HD].rearrange("p t h d -> p (t h) d"),
                            in0=desk_bank[DESK["v"]][:, :].rearrange("p (a d) -> p a d", d=HD),
                            scalar=scales[:, 2:3], in1=b_v_all.rearrange("p (a d) -> p a d", d=HD),
                            op0=ALU.mult, op1=ALU.add).then_inc(emptied[DESK["v"]], 1)
                    if s == 18 and T:
                        wait_filled(dve, b, "proj", inner)
                        wait(dve, xb_ready, b)
                        wait(dve, mixed, 16 * (b - 1))
                        V.scalar_tensor_tensor(
                            out=x1[:, :, :].rearrange("p t d -> p (t d)"), in0=desk_bank[DESK["proj"]][:, :],
                            scalar=scales[:, 3:4], in1=x_bias[:, :, :].rearrange("p t d -> p (t d)"),
                            op0=ALU.mult, op1=ALU.add).then_inc(emptied[DESK["proj"]], 1)
                    if s == 19 and T:
                        wait_emptied(dve, b, "proj", inner)
                        for t in range(QT):
                            last = V.bn_stats(stats2[:, t, :], x1[:, t, :])
                        last.then_inc(ln2, 1)
                    if s == 20 and T:
                        for t in range(QT):
                            last = V.bn_aggr(mean_var2[:, t, :], stats2[:, t, :])
                        last.then_inc(ln2, 1)
                    if s == 21 and T:
                        wait(dve, ln2, 3 * (b - 1) + 2)
                        V.tensor_scalar(var_eps2[:, :], mean_var2[:, :, 1], EPS, None, ALU.add).then_inc(ln2, 1)
                    if s == 25 and A:
                        norm_ctx(b, 0, b, inner)
                    if s == 32 and T:
                        wait_filled(dve, b, "logits", inner)
                        V.tensor_tensor(logits[:, :, :],
                                        desk_bank[DESK["logits"]][:, 0:QT * TOPW].rearrange("p (t e) -> p t e", e=TOPW),
                                        gate_b_all.unsqueeze(1).to_broadcast([P, QT, TOPW]),
                                        ALU.add).then_inc(emptied[DESK["logits"]], 1)
                    if s == 33 and T:
                        wait_emptied(dve, b, "logits", inner)
                        step(1, V.reduce_max(g4[:, 0, :], logits[:, :, :], AX_X, negate=True))
                        after(1)
                        step(2, V.tensor_tensor(g10[:, 0, :, :], logits[:, :, :], wide(g4[:, 0, :]), ALU.add))
                    if s == 37 and T:
                        wait(dve, gate_exp, b)
                        step(3, V.reduce_sum(g4[:, 1, :], g10[:, 1, :, :], AX_X))
                        after(3)
                        step(4, V.reciprocal(g4[:, 2, :], g4[:, 1, :]))
                    if s == 38 and T:
                        after(4)
                        step(5, V.tensor_tensor(g10[:, 2, :, :], g10[:, 1, :, :], wide(g4[:, 2, :]), ALU.mult))
                        after(5)
                        step(6, V.reduce_max(g4[:, 3, :], g10[:, 2, :, :], AX_X))
                    if s == 39 and T:
                        after(6)
                        step(7, V.tensor_tensor(g10[:, 3, :, :], g10[:, 2, :, :], wide(g4[:, 3, :]), ALU.subtract))
                        after(7)
                        step(8, V.scalar_tensor_tensor(out=g10[:, 4, :, :], in0=g10[:, 3, :, :], scalar=0.0,
                                                       in1=order[:, :, :], op0=ALU.is_ge, op1=ALU.mult))
                    if s == 40 and T:
                        after(8)
                        step(9, V.reduce_max(g4[:, 4, :], g10[:, 4, :, :], AX_X))
                        after(9)
                        step(10, V.tensor_tensor(g10[:, 5, :, :], g10[:, 4, :, :], wide(g4[:, 4, :]), ALU.is_equal))
                    if s == 41 and T:
                        after(10)
                        step(11, V.scalar_tensor_tensor(out=g10[:, 6, :, :], in0=g10[:, 5, :, :], scalar=-2.0,
                                                        in1=g10[:, 2, :, :], op0=ALU.mult, op1=ALU.add))
                        after(11)
                        step(12, V.reduce_max(g4[:, 5, :], g10[:, 6, :, :], AX_X))
                    if s == 41 and A:
                        norm_ctx(b, 1, b, inner)
                    if s == 42 and T:
                        after(12)
                        step(13, V.tensor_tensor(g10[:, 7, :, :], g10[:, 6, :, :], wide(g4[:, 5, :]), ALU.subtract))
                        after(13)
                        step(14, V.scalar_tensor_tensor(out=g10[:, 8, :, :], in0=g10[:, 7, :, :], scalar=0.0,
                                                        in1=order[:, :, :], op0=ALU.is_ge, op1=ALU.mult))
                    if s == 43 and T:
                        after(14)
                        step(15, V.reduce_max(g4[:, 6, :], g10[:, 8, :, :], AX_X))
                        after(15)
                        step(16, V.tensor_tensor(g10[:, 9, :, :], g10[:, 8, :, :], wide(g4[:, 6, :]), ALU.is_equal))
                        after(16)
                        step(17, V.tensor_tensor(chosen[:, :, :], g10[:, 5, :, 0:NE], g10[:, 9, :, 0:NE], ALU.add))
                    if s == 44 and T:
                        after(17)
                        step(18, V.tensor_tensor(true_w[:, :, :], g10[:, 2, :, 0:NE], chosen[:, :, :], ALU.mult))
                        after(18)
                        step(19, V.reduce_sum(g4[:, 7, :], true_w[:, :, :], AX_X))
                        after(19)
                        step(20, V.scalar_tensor_tensor(out=g4[:, 8, :], in0=g4[:, 7, :], scalar=0.0,
                                                        in1=g4[:, 7, :], op0=ALU.is_le, op1=ALU.add))
                    if s == 45 and T:
                        after(20)
                        step(21, V.reciprocal(g4[:, 9, :], g4[:, 8, :]))
                        after(21)
                        step(22, V.tensor_tensor(combine_w[:, :, :], true_w[:, :, :],
                                                 g4[:, 9, :].unsqueeze(2).to_broadcast([P, QT, NE]), ALU.mult))
                    if s == 46 and T:
                        after(22)
                    if s in WEIGH and T:
                        weigh(b, *WEIGH[s], inner)
                    if s == 58 and A:
                        norm_ctx(b, 2, b, inner)

            bodies(dve, body)

        @block.tensor
        def _(pe):
            T_ = nc.tensor
            pe.wait_ge(pool_setup, POOL_SETUP_EB)
            pe.wait_ge(w_loaded, W_DMAS * 16)
            pe.wait_ge(dve_setup, DVE_SETUP)
            pe.wait_ge(eb_loaded, 16)

            def scores_t(b, s, par):
                g, t, c = s // 16, s % 16 // 4, s % 4
                j, h = head_of(g, c)
                if s % 16 == 0:
                    wait(pe, rows_max, 32 * (4 * b + g + 1))
                wait(pe, exp_done, SLOTS * b + s - 1)
                r = slice(64 * h, 64 * h + ROWS_ST)
                T_.matmul(st_bank[s % 2][:, :], k_rows[par][r, j, P * t:P * t + P], q_rows[par][r, j, :],
                          start=True, stop=True).then_inc(st_filled, 1)

            def scores(b, s, par):
                u = SLOTS * b + s + 32
                g, t, c = (s // 16 + 2) % 4, s % 16 // 4, (s % 4) ^ 1
                j, h = head_of(g, c)
                if s == 32:
                    wait(pe, rows_qk, 16 * LOADS * (b + 2))
                wait(pe, max_done, u - 1)
                r = slice(64 * h, 64 * h + ROWS_QK)
                T_.matmul(s_bank[s % 2][:, :], q_rows[par][r, j, P * t:P * t + P], k_rows[par][r, j, :],
                          start=True, stop=True).then_inc(s_filled, 1)

            def values(b, n, par):
                g, t = n // 4, n % 4
                wait(pe, exp_done, SLOTS * b + 4 * n + 4)
                if t == 0:
                    wait(pe, pv_taken, 4 * b + g)
                for c in range(4):
                    last = T_.matmul(pv_bank[32 * c:32 * c + 32, :], v_ones[par][:, t, 4 * g + c, :],
                                     probs[:, 4 * (n % 2) + c, :], start=t == 0, stop=t == QT - 1)
                last.then_inc(pv_done, 1)

            def task(b, name, par, inner):
                desk, bank = DESK[name], desk_bank[DESK[name]]
                wait(pe, emptied[desk], place(b, name, inner))
                if name.startswith("rows"):
                    g = int(name[-1])
                    n = 4 * (b + (g == 0)) + g
                    wait(pe, max_split, 4 * n + 4)
                    rows = bank[0:12, 0:S // 2].bitcast(BF16)
                    for t in range(QT):
                        last = T_.transpose(rows[:, P * t:P * t + P], max_parts[:, g % 2, t, :], identity_bf[:, :])
                elif name == "xn_t":
                    wait(pe, xn_ready, b + 2)
                    for t in range(QT):
                        last = T_.transpose(bank[:, P * t:P * t + P], xn[:, t, :], identity[:, :])
                elif name in "qk":
                    wait_emptied(pe, b, "xn_t", inner)
                    last = T_.matmul(bank[:, :], w_qk_t[:, "qk".index(name), :], xn_t[:, :], start=True, stop=True)
                elif name == "v":
                    for t in range(QT):
                        last = T_.matmul(bank[:, P * t:P * t + P], xn_t[:, P * t:P * t + P], w_v_t,
                                         start=True, stop=True)
                elif name in ("ctx0", "ctx1", "ctx2", "ctx3"):
                    g = int(name[-1])
                    wait(pe, pv_taken, 4 * (b - (g == 3)) + g + 1)
                    for t in range(QT):
                        last = T_.transpose(bank[:, P * t:P * t + P], ctx_raw[:, g % 2, P * t:P * t + P],
                                            identity[:, :])
                elif name == "ctx_t":
                    wait_emptied(pe, b, "ctx3", inner)
                    for t in range(QT):
                        last = T_.transpose(bank[:, P * t:P * t + P], ctx_tok[:, t, :], identity[:, :])
                elif name == "proj":
                    wait_emptied(pe, b, "ctx_t", inner)
                    for t in range(QT):
                        last = T_.matmul(bank[:, P * t:P * t + P], ctx_t[:, P * t:P * t + P], w_o_t,
                                         start=True, stop=True)
                elif name == "xn2_t":
                    wait(pe, xn2_ready, b)
                    for t in range(QT):
                        last = T_.transpose(bank[:, P * t:P * t + P], xn2[:, t, :], identity[:, :])
                elif name == "logits":
                    wait_emptied(pe, b, "xn2_t", inner)
                    for t in range(QT):
                        last = T_.matmul(bank[:, TOPW * t:TOPW * t + TOPW], xn2_t[:, P * t:P * t + P], gate_t,
                                         start=True, stop=True)
                else:
                    t, half = int(name[1]), "ab".index(name[2])
                    T_.matmul(bank[:, :], xn2_t[:, P * t:P * t + P],
                              w_exp[:, 512 * half:512 * half + 512], start=True, stop=False)
                    last = T_.matmul(bank[:, :], ones3[:, :], eb_rows[:, 512 * half:512 * half + 512],
                                     start=False, stop=True)
                last.then_inc(filled[desk], 1)

            def body(b, par, inner):
                here = dict(zip("AFT", parts_of(b, inner)))
                for s in range(SLOTS):
                    if here["A"]:
                        scores_t(b, s, par)
                    if s < 32 and here["A"]:
                        scores(b, s, par)
                    if s >= 32 and here["F"]:
                        scores(b, s, 1 - par)
                    if s % 4 == 3:
                        if s > 3 and here["A"]:
                            values(b, s // 4 - 1, par)
                        if s == 3 and here["T"]:
                            values(b - 1, 15, 1 - par)
                    if s in PE_SLOT and here[WHO[PE_SLOT[s]]]:
                        task(b, PE_SLOT[s], par, inner)

            bodies(pe, body)


def kernel(**inputs):
    import concourse.bacc as _bacc
    from concourse.bass_utils import run_bass_kernel_spmd as _run

    a = {name[3:]: np.asarray(v) for name, v in inputs.items()}
    qk_order = np.arange(P).reshape(2, JP, HD).transpose(0, 2, 1).ravel()
    v_order = np.arange(P).reshape(2, JP, HD).transpose(1, 0, 2).ravel()
    weights = np.concatenate([a["attn_w_q"].T[:, qk_order], a["attn_w_k"].T[:, qk_order], a["attn_w_v"].T[:, v_order],
                              a["attn_w_o"].T[v_order], a["ffn_gate_w"].T], axis=1)
    scalars = [a[f"attn_s_{n}"].reshape(1) for n in "qkvo"]
    arrays = {
        "x": a["attn_x"],
        "weights": weights,
        "experts": a["ffn_expert_w"].transpose(1, 0, 2).reshape(P, NE * P),
        "vectors": np.concatenate([np.tile(a["attn_b_v"][v_order], 4), a["attn_b_o"], a["ffn_gate_b"]] + scalars),
        "qk_biases": np.stack([a["attn_b_q"][qk_order], a["attn_b_k"][qk_order]], axis=1),
        "expert_b": a["ffn_expert_b"],
    }
    arrays = {name: np.ascontiguousarray(v) for name, v in arrays.items()}
    nc = _bacc.Bacc("TRN2", target_bir_lowering=False, num_devices=1)
    args = [nc.dram_tensor(name, v.shape, mybir.dt.from_np(v.dtype), kind="ExternalInput").ap()
            for name, v in arrays.items()]
    args.append(nc.dram_tensor("layer_out", arrays["x"].shape, F32, kind="ExternalOutput").ap())
    build(nc, *args)
    return _run(nc, [arrays], core_ids=[0]).results[0]["layer_out"]
```

```python
from contextlib import ExitStack

import numpy as np

import concourse.bass as bass
from concourse import mybir

F32 = mybir.dt.float32
BF16 = mybir.dt.bfloat16
ALU = mybir.AluOpType
ACT = mybir.ActivationFunctionType
AX_X = mybir.AxisListType.X

P = 128
EPS = 1e-5
HEADS, HD = 16, 8
TOPW = 10
NE = 8
ROWS_QK = 6 * HD
ROW_MAX = P - 3
SLOTS = 64
PV_PHASE = 1
GATE_STEPS = 22
W_DMAS = 5
POOL_SETUP = 6
DVE_SETUP = 2
LOADS = 12

BF16_ONES = float(np.array([0x3F803F80], np.uint32).view(np.float32)[0])

Q_TERMS = (0, 0, 0, 1, 1, 2)
K_TERMS = (0, 1, 2, 0, 1, 0)

TASKS = (
    (5, "ctx3", "T"), (6, "rows1", "A"), (8, "xn_t", "F"), (9, "ctx_t", "T"), (11, "q", "F"), (13, "proj", "T"),
    (15, "k", "F"), (17, "v", "F"), (21, "rows2", "A"), (22, "ctx0", "A"), (25, "xn2_t", "T"), (27, "logits", "T"),
    (37, "rows3", "A"), (38, "ctx1", "A"), (40, "e0a", "T"), (42, "e0b", "T"), (46, "e1a", "T"), (48, "e1b", "T"),
    (50, "e2a", "T"), (52, "e2b", "T"), (54, "rows0", "F"), (55, "ctx2", "A"), (58, "e3a", "T"), (60, "e3b", "T"),
)
ACT_AT = {"pv3": 3, "rows1": 8, "xn_t": 9, "ctx_t": 11, "q": 12, "k": 16, "pv0": 19, "rows2": 22, "xn2_t": 26,
          "gate": 32, "pv1": 35, "rows3": 38, "pv2": 51, "rows0": 56}
DVE_AT = {"stats": 0, "aggr": 1, "var": 2, "ctx3": 7, "proj": 15, "stats2": 16, "aggr2": 17, "var2": 18, "v": 19,
          "ctx0": 24, "logits": 29, "gate1": 30, "gate3": 34, "gate5": 35, "gate7": 36, "gate9": 37, "gate11": 38,
          "ctx1": 39, "gate13": 40, "gate15": 41, "gate18": 42, "gate21": 43,
          "e0a": 44, "e0b": 45, "e1a": 48, "e1b": 50, "e2a": 52, "e2b": 54, "ctx2": 57, "e3a": 60, "e3b": 62}
DESK = {name: n % 2 for n, (_, name, _) in enumerate(TASKS)}
PE_SLOT = {slot: name for slot, name, _ in TASKS}
WHO = {name: who for _, name, who in TASKS}


W_QK, W_V, W_O, W_GATE, W_END = 0, 2 * P, 3 * P, 4 * P, 4 * P + TOPW
V_BV, V_BO, V_BG, V_SCALES, V_END = 0, 4 * P, 5 * P, 5 * P + TOPW, 5 * P + TOPW + 4


def build(nc, x, weights, experts, vectors, qk_biases, expert_b, out):
    B, S, D = x.shape
    QT = S // P
    assert D == P and S == 512 and HEADS * HD == D and experts.shape[1] == NE * D

    def present(b):
        return {"A": 0 <= b < B, "F": b + 1 < B, "T": b >= 1}

    def uses(b, desk):
        return sum(present(b)[who] for _, name, who in TASKS if DESK[name] == desk)

    def place(b, name, inner):
        desk = DESK[name]
        first = 1 if inner else b
        here = present(first)
        n = sum(uses(bb, desk) for bb in range(-1, first))
        for _, other, who in TASKS:
            if other == name:
                break
            n += here[who] and DESK[other] == desk
        return n + (b - 1) * uses(1, desk) if inner else n

    ctx = ExitStack()
    with ctx:
        def sb(name, shape, dt=F32):
            return ctx.enter_context(nc.sbuf_tensor(name, shape, dt))

        def ps(name):
            return ctx.enter_context(nc.psum_tensor(name, [P, 512], F32))

        def sem(name):
            return ctx.enter_context(nc.semaphore(name))

        st_bank = [ps(f"st_bank{i}") for i in range(2)]
        s_bank = [ps(f"s_bank{i}") for i in range(3)]
        pv_bank = ps("pv_bank")
        desk_bank = [ps(f"desk_bank{i}") for i in range(2)]

        identity = sb("identity", [P, P])
        identity_bf = sb("identity_bf", [P, P], BF16)
        w_all = sb("w_all", [P, W_END])
        w_qk_t = w_all[:, W_QK:W_V].rearrange("i (n o) -> i n o", n=2)
        w_v_t = w_all[:, W_V:W_O]
        w_o_t = w_all[:, W_O:W_GATE]
        gate_t = w_all[:, W_GATE:W_END]
        w_exp = sb("w_exp", [P, NE * P])
        vec_all = sb("vec_all", [P, V_END])
        b_v_all = vec_all[:, V_BV:V_BO]
        b_o_all = vec_all[:, V_BO:V_BG]
        gate_b_all = vec_all[:, V_BG:V_SCALES]
        scales = vec_all[:, V_SCALES:V_END]
        eb_rows = sb("eb_rows", [3, NE * P], BF16)
        ones3 = sb("ones3", [3, P], BF16)
        qk_scale = sb("qk_scale", [P, 2])
        qk_bias_nat = sb("qk_bias_nat", [P, 2])
        qk_bias = sb("qk_bias", [P, 2])
        neg_half = sb("neg_half", [P, QT])
        zeros = sb("zeros", [P, QT, 4])
        order = sb("order", [P, QT, TOPW])

        x_all = sb("x_all", [P, B * QT, P])
        stats = sb("stats", [P, QT, 6])
        mean_var = sb("mean_var", [P, QT, 2])
        var_eps = sb("var_eps", [P, QT])
        rstd = sb("rstd", [P, QT])
        x_centred = sb("x_centred", [P, QT, P])
        xn = sb("xn", [P, QT, P])
        xn_t = sb("xn_t", [P, S])
        qk_full = sb("qk_full", [P, 2, S])
        qk_rest = sb("qk_rest", [P, 2, S])
        qk_parts = sb("qk_parts", [P, 2, 3, S], BF16)
        q_rows = [sb(f"q_rows{i}", [P, HEADS, S], BF16) for i in range(2)]
        k_rows = [sb(f"k_rows{i}", [P, HEADS, S], BF16) for i in range(2)]
        v_ones = [sb(f"v_ones{i}", [P, QT, HEADS, 32]) for i in range(2)]
        neg_max = sb("neg_max", [P, 2, QT, 4])
        neg_rest = sb("neg_rest", [P, QT, 4])
        max_parts = sb("max_parts", [P, 2, QT, 12], BF16)
        max_rows = sb("max_rows", [12, 2, S], BF16)
        probs = sb("probs", [P, 8, S])
        ctx_raw = sb("ctx_raw", [P, 2, S])
        inv_sum = sb("inv_sum", [P, QT, 4])
        ctx_tok = sb("ctx_tok", [P, QT, P])
        ctx_t = sb("ctx_t", [P, S])
        x_bias = sb("x_bias", [P, QT, P])
        x1 = sb("x1", [P, QT, P])
        stats2 = sb("stats2", [P, QT, 6])
        mean_var2 = sb("mean_var2", [P, QT, 2])
        var_eps2 = sb("var_eps2", [P, QT])
        rstd2 = sb("rstd2", [P, QT])
        x1_centred = sb("x1_centred", [P, QT, P])
        xn2 = sb("xn2", [P, QT, P])
        xn2_t = sb("xn2_t", [P, S])
        logits = sb("logits", [P, QT, TOPW])
        g4 = sb("g4", [P, 10, QT])
        g10 = sb("g10", [P, 10, QT, TOPW])
        true_w = sb("true_w", [P, QT, NE])
        chosen = sb("chosen", [P, QT, NE])
        combine_w = sb("combine_w", [P, QT, NE])
        prod = sb("prod", [P, 2, NE, P])
        eb_row = prod[0:1, 0, :, :].rearrange("p e d -> p (e d)")
        eb_rest = prod[0:1, 1, :, :].rearrange("p e d -> p (e d)")
        eb_parts = sb("eb_parts", [1, 3, NE * P], BF16)
        sum4 = sb("sum4", [P, 4, P])
        sum2 = sb("sum2", [P, 2, P])
        sum1 = sb("sum1", [P, P])
        y = sb("y", [P, QT, P])

        w_loaded = sem("w_loaded")
        x0_loaded = sem("x0_loaded")
        x_loaded = sem("x_loaded")
        pool_setup = sem("pool_setup")
        dve_setup = sem("dve_setup")
        eb_split = sem("eb_split")
        eb_loaded = sem("eb_loaded")
        rows_cleared = [sem(f"rows_cleared{i}") for i in range(2)]
        filled = [sem("desk0_filled"), sem("desk1_filled")]
        emptied = [sem("desk0_emptied"), sem("desk1_emptied")]
        ln1 = sem("ln1")
        ln1_centred = sem("ln1_centred")
        xn_ready = sem("xn_ready")
        qk_split = sem("qk_split")
        rows_qk = sem("rows_qk")
        s_filled = sem("s_filled")
        max_done = sem("max_done")
        max_split = sem("max_split")
        rows_max = sem("rows_max")
        st_filled = sem("st_filled")
        exp_done = sem("exp_done")
        pv_done = sem("pv_done")
        pv_taken = sem("pv_taken")
        inv_done = sem("inv_done")
        xb_ready = sem("xb_ready")
        x1_ready = sem("x1_ready")
        ln2 = sem("ln2")
        ln2_centred = sem("ln2_centred")
        xn2_ready = sem("xn2_ready")
        gate = sem("gate")
        gate_exp = sem("gate_exp")
        mixed = sem("mixed")
        y_free = sem("y_free")

        block = ctx.enter_context(nc.Block())

        def wait(eng, semaphore, count):
            if not (isinstance(count, int) and count <= 0):
                eng.wait_ge(semaphore, count)

        def wait_filled(eng, b, name, inner):
            wait(eng, filled[DESK[name]], place(b, name, inner) + 1)

        def wait_emptied(eng, b, name, inner):
            wait(eng, emptied[DESK[name]], place(b, name, inner) + 1)

        def bodies(eng, body):
            body(-1, 1, False)
            body(0, 0, False)
            with eng.Fori(1, B - 2, 2) as b:
                body(b, 1, True)
                body(b + 1, 0, True)
            body(B - 1, 1, False)
            body(B, 0, False)

        def clear_rows(eng, par):
            eng.memset(q_rows[par][:, :, :].bitcast(F32), 0.0).then_inc(rows_cleared[par], 1)
            eng.memset(k_rows[par][:, :, :].bitcast(F32), BF16_ONES).then_inc(rows_cleared[par], 1)

        def parts_of(b, inner):
            return (True, True, True) if inner else tuple(present(b)[w] for w in "AFT")

        @block.sync
        def _(sync):
            x_v = x.rearrange("b (p t) d -> p b (t d)", p=P)
            out_v = out.rearrange("b (p t) d -> p b (t d)", p=P)
            sync.dma_start(x_all[:, 0:QT, :], x_v[:, 0, :]).then_inc(x0_loaded, 16)
            sync.dma_start(w_all[:, :], weights).then_inc(w_loaded, 16)
            sync.dma_start(vec_all[:, :], vectors.partition_broadcast(P)).then_inc(w_loaded, 16)
            sync.dma_start(qk_bias_nat[:, :], qk_biases).then_inc(w_loaded, 16)
            sync.dma_start(eb_row, expert_b.rearrange("(a e) h -> a (e h)", a=1)).then_inc(w_loaded, 16)
            sync.dma_start(w_exp[:, :], experts).then_inc(w_loaded, 16)
            for b in range(1, B):
                sync.dma_start(x_all[:, b * QT:(b + 1) * QT, :], x_v[:, b, :]).then_inc(x_loaded, 16)

            def put_max_rows(b, g, par, inner):
                name = f"rows{g}"
                wait_emptied(sync, b - (g == 0), name, inner)
                sync.dma_start(q_rows[par][ROW_MAX:P, 4 * g:4 * g + 4, :], max_rows[:, g % 2, :]).then_inc(rows_max, 16)

            def body(b, par, inner):
                A, F, T = parts_of(b, inner)
                if not inner and b == 0:
                    sync.wait_ge(eb_split, 4)
                    sync.dma_start(eb_rows[:, :], eb_parts[:, :, :]).then_inc(eb_loaded, 16)
                if A:
                    put_max_rows(b, 1, par, inner)
                if F:
                    if not inner:
                        wait(sync, rows_cleared[1 - par], 2)
                    for n, (rows, terms) in enumerate(((q_rows[1 - par], Q_TERMS), (k_rows[1 - par], K_TERMS))):
                        for part in range(3):
                            if part == 0:
                                wait_emptied(sync, b, "qk"[n], inner)
                            else:
                                wait(sync, qk_split, 6 * (b + 1) + 3 * n + (1, 3)[part - 1])
                            for t in (t for t in range(6) if terms[t] == part):
                                sync.dma_start(rows[HD * t:HD * t + HD, :, :], qk_parts[:, n, part, :])\
                                    .then_inc(rows_qk, 16)
                if A:
                    put_max_rows(b, 2, par, inner)
                    put_max_rows(b, 3, par, inner)
                if F:
                    put_max_rows(b + 1, 0, 1 - par, inner)
                if T:
                    wait(sync, mixed, 1 + 16 * b)
                    sync.dma_start(out_v[:, bass.ds(b - 1, 1), :], y[:, :, :].rearrange("p (a t) d -> p a (t d)", a=1))\
                        .then_inc(y_free, 16)

            bodies(sync, body)
            sync.wait_ge(y_free, 16 * (B + 1))

        @block.gpsimd
        def _(pool):
            pool.memset(identity[:, :], 0.0).then_inc(pool_setup, 1)
            pool.wait_ge(pool_setup, 1)
            pool.affine_select(out=identity[:, :], in_=identity[:, :], compare_op=ALU.not_equal, fill=1.0,
                               base=0, pattern=[[-1, P]], channel_multiplier=1).then_inc(pool_setup, 1)
            pool.wait_ge(pool_setup, 2)
            pool.tensor_copy(identity_bf[:, :], identity[:, :]).then_inc(pool_setup, 1)
            pool.memset(ones3[:, :], 1.0).then_inc(pool_setup, 1)
            for n in range(TOPW):
                last = pool.memset(order[:, :, n:n + 1], float(TOPW - n))
            last.then_inc(pool_setup, 1)
            pool.memset(zeros[:, :, :], 0.0)
            pool.memset(neg_half[:, :], -0.5).then_inc(pool_setup, 1)
            pool.wait_ge(pool_setup, POOL_SETUP)

            def split_biases():
                pool.wait_ge(w_loaded, W_DMAS * 16)
                pool.tensor_copy(eb_parts[:, 0, :], eb_row).then_inc(eb_split, 1)
                pool.wait_ge(eb_split, 1)
                pool.tensor_tensor(eb_parts[:, 1, :], eb_row, eb_parts[:, 0, :], ALU.subtract).then_inc(eb_split, 1)
                pool.tensor_tensor(eb_rest, eb_row, eb_parts[:, 0, :], ALU.subtract).then_inc(eb_split, 1)
                pool.wait_ge(eb_split, 3)
                pool.tensor_tensor(eb_parts[:, 2, :], eb_rest, eb_parts[:, 1, :], ALU.subtract).then_inc(eb_split, 1)

            def split_max(b, g):
                n = 4 * b + g
                r = g % 2
                whole = neg_max[:, r, :, :]

                def part(k):
                    return max_parts[:, r, :, 4 * k:4 * k + 4]
                wait(pool, max_done, 16 * (n + 1))
                pool.tensor_tensor(part(0), whole, zeros[:, :, :], ALU.add).then_inc(max_split, 1)
                pool.wait_ge(max_split, 4 * n + 1)
                pool.tensor_tensor(part(1), whole, part(0), ALU.subtract).then_inc(max_split, 1)
                pool.tensor_tensor(neg_rest[:, :, :], whole, part(0), ALU.subtract).then_inc(max_split, 1)
                pool.wait_ge(max_split, 4 * n + 3)
                pool.tensor_tensor(part(2), neg_rest[:, :, :], part(1), ALU.subtract).then_inc(max_split, 1)

            def per_token(v):
                return v.unsqueeze(2).to_broadcast([P, QT, P])

            def mix(b, t):
                n = 1 + 16 * (b - 1) + 4 * t
                if t == 0:
                    wait(pool, y_free, 16 * b)
                pool.tensor_tensor(sum4[:, :, :], prod[:, t % 2, 0:4, :], prod[:, t % 2, 4:8, :], ALU.add).then_inc(mixed, 1)
                pool.wait_ge(mixed, n + 1)
                pool.tensor_tensor(sum2[:, :, :], sum4[:, 0:2, :], sum4[:, 2:4, :], ALU.add).then_inc(mixed, 1)
                pool.wait_ge(mixed, n + 2)
                pool.tensor_tensor(sum1[:, :], sum2[:, 0, :], sum2[:, 1, :], ALU.add).then_inc(mixed, 1)
                pool.wait_ge(mixed, n + 3)
                pool.tensor_tensor(y[:, t, :], sum1[:, :], x1[:, t, :], ALU.add).then_inc(mixed, 1)

            def body(b, par, inner):
                A, F, T = parts_of(b, inner)
                if not inner and b == 0:
                    pool.wait_ge(x_loaded, 16 * (B - 1))
                if A:
                    split_max(b, 1)
                if F:
                    wait(pool, ln1, 3 * (b + 1) + 2)
                    pool.tensor_tensor(x_centred[:, :, :], x_all[:, bass.ts(b + 1, QT), :],
                                       per_token(mean_var[:, :, 0]), ALU.subtract).then_inc(ln1_centred, 1)
                    wait(pool, ln1, 3 * (b + 1) + 3)
                    pool.tensor_tensor(rstd[:, :], var_eps[:, :], neg_half[:, :], ALU.pow).then_inc(ln1_centred, 1)
                    wait(pool, ln1_centred, 2 * (b + 2))
                    pool.tensor_tensor(xn[:, :, :], x_centred[:, :, :], per_token(rstd[:, :]), ALU.mult)\
                        .then_inc(xn_ready, 1)
                if T:
                    pool.tensor_tensor(x_bias[:, :, :], x_all[:, bass.ts(b - 1, QT), :],
                                       b_o_all.unsqueeze(1).to_broadcast([P, QT, P]), ALU.add)\
                        .then_inc(xb_ready, 1)
                if F:
                    for n, name in enumerate("qk"):
                        c = 6 * (b + 1) + 3 * n
                        wait_emptied(pool, b, name, inner)
                        pool.tensor_tensor(qk_parts[:, n, 1, :], qk_full[:, n, :], qk_parts[:, n, 0, :],
                                           ALU.subtract).then_inc(qk_split, 1)
                        pool.tensor_tensor(qk_rest[:, n, :], qk_full[:, n, :], qk_parts[:, n, 0, :],
                                           ALU.subtract).then_inc(qk_split, 1)
                        pool.wait_ge(qk_split, c + 2)
                        pool.tensor_tensor(qk_parts[:, n, 2, :], qk_rest[:, n, :], qk_parts[:, n, 1, :],
                                           ALU.subtract).then_inc(qk_split, 1)
                if not inner and b == -1:
                    clear_rows(pool, 1)
                    split_biases()
                if A:
                    split_max(b, 2)
                if T:
                    wait(pool, ln2, 3 * (b - 1) + 2)
                    pool.tensor_tensor(x1_centred[:, :, :], x1[:, :, :],
                                       per_token(mean_var2[:, :, 0]), ALU.subtract).then_inc(ln2_centred, 1)
                    wait(pool, ln2, 3 * (b - 1) + 3)
                    pool.tensor_tensor(rstd2[:, :], var_eps2[:, :], neg_half[:, :], ALU.pow).then_inc(ln2_centred, 1)
                    wait(pool, ln2_centred, 2 * b)
                    pool.tensor_tensor(xn2[:, :, :], x1_centred[:, :, :], per_token(rstd2[:, :]), ALU.mult)\
                        .then_inc(xn2_ready, 1)
                if A:
                    split_max(b, 3)
                if F:
                    split_max(b + 1, 0)
                for t in range(QT):
                    if T:
                        wait_emptied(pool, b, f"e{t}b", inner)
                        mix(b, t)

            pool.memset(sum1[:, :], 0.0).then_inc(mixed, 1)
            pool.memset(y[:, :, :], 0.0).then_inc(y_free, 16)
            pool.wait_ge(x0_loaded, 16)
            bodies(pool, body)

        @block.scalar
        def _(act):
            def take_pv(b, g):
                n = 4 * b + g
                wait(act, pv_done, 4 * n + 4)
                act.copy(ctx_raw[:, g % 2, :], pv_bank[:, :]).then_inc(pv_taken, 1)

            def take_rows(b, name, inner):
                g = int(name[-1])
                wait_filled(act, b, name, inner)
                act.copy(max_rows[:, g % 2, :], desk_bank[DESK[name]][0:12, 0:S // 2].bitcast(BF16))\
                    .then_inc(emptied[DESK[name]], 1)

            def take(b, name, dst, inner):
                wait_filled(act, b, name, inner)
                act.copy(dst[:, :], desk_bank[DESK[name]][:, :]).then_inc(emptied[DESK[name]], 1)

            def body(b, par, inner):
                A, F, T = parts_of(b, inner)
                for s in range(SLOTS):
                    if A:
                        a = SLOTS * b + s
                        wait(act, st_filled, a + 1)
                        if s % 4 == 0:
                            wait(act, pv_done, 16 * b + s // 4 - 1)
                        act.activation(probs[:, s % 8, :], st_bank[s % 2][:, :], ACT.Exp).then_inc(exp_done, 1)
                    if s == ACT_AT["pv3"] and T:
                        take_pv(b - 1, 3)
                    if s == ACT_AT["rows1"] and A:
                        take_rows(b, "rows1", inner)
                    if s == ACT_AT["xn_t"] and F:
                        take(b, "xn_t", xn_t, inner)
                    if s in (ACT_AT["q"], ACT_AT["k"]) and F:
                        n, name = (0, "q") if s == ACT_AT["q"] else (1, "k")
                        bank = desk_bank[DESK[name]]
                        wait_filled(act, b, name, inner)
                        act.activation(qk_parts[:, n, 0, :], bank[:, :], ACT.Identity,
                                       scale=qk_scale[:, n:n + 1], bias=qk_bias[:, n:n + 1])
                        act.activation(qk_full[:, n, :], bank[:, :], ACT.Identity,
                                       scale=qk_scale[:, n:n + 1], bias=qk_bias[:, n:n + 1])\
                            .then_inc(emptied[DESK[name]], 1)
                    if s == ACT_AT["ctx_t"] and T:
                        take(b, "ctx_t", ctx_t, inner)
                    if s == ACT_AT["pv0"] and A:
                        take_pv(b, 0)
                    if s == ACT_AT["rows2"] and A:
                        take_rows(b, "rows2", inner)
                    if s == ACT_AT["xn2_t"] and T:
                        take(b, "xn2_t", xn2_t, inner)
                    if s == ACT_AT["gate"] and T:
                        wait(act, gate, GATE_STEPS * (b - 1) + 2)
                        act.activation(g10[:, 1, :, :], g10[:, 0, :, :], ACT.Exp).then_inc(gate_exp, 1)
                    if s == ACT_AT["pv1"] and A:
                        take_pv(b, 1)
                    if s == ACT_AT["rows3"] and A:
                        take_rows(b, "rows3", inner)
                    if s == ACT_AT["pv2"] and A:
                        take_pv(b, 2)
                    if s == ACT_AT["rows0"] and F:
                        take_rows(b, "rows0", inner)

            act.wait_ge(dve_setup, DVE_SETUP)
            bodies(act, body)

        @block.vector
        def _(dve):
            for i in range(2):
                nc.vector.memset(v_ones[i][:, :, :, HD + 1:32], 0.0)
                last = nc.vector.memset(v_ones[i][:, :, :, HD:HD + 1], 1.0)
            last.then_inc(dve_setup, 1)
            dve.wait_ge(w_loaded, W_DMAS * 16)
            root = float(1.0 / np.sqrt(np.float32(HD)))
            nc.vector.tensor_scalar(qk_scale[:, 0:1], scales[:, 0:1], root, None, ALU.mult)
            nc.vector.tensor_copy(qk_scale[:, 1:2], scales[:, 1:2])
            nc.vector.tensor_scalar(qk_bias[:, 0:1], qk_bias_nat[:, 0:1], root, None, ALU.mult)
            nc.vector.tensor_copy(qk_bias[:, 1:2], qk_bias_nat[:, 1:2]).then_inc(dve_setup, 1)
            dve.wait_ge(x0_loaded, 16)

            def norm_ctx(b, g, body_b, inner):
                n, name = 4 * b + g, f"ctx{g}"
                wait_filled(dve, body_b, name, inner)
                bank = desk_bank[DESK[name]][:, :].rearrange("p (t c k) -> p t c k", t=QT, k=32)
                nc.vector.reciprocal(inv_sum[:, :, :], bank[:, :, :, HD]).then_inc(inv_done, 1)
                wait(dve, inv_done, n + 1)
                nc.vector.tensor_tensor(
                    ctx_tok[:, :, 32 * g:32 * g + 32].rearrange("p t (c d) -> p t c d", d=HD),
                    bank[:, :, :, 0:HD], inv_sum[:, :, :].unsqueeze(3).to_broadcast([P, QT, 4, HD]),
                    ALU.mult).then_inc(emptied[DESK[name]], 1)

            def weigh(b, name, inner):
                t, half = int(name[1]), "ab".index(name[2])
                wait_filled(dve, b, name, inner)
                if t >= 2 and half == 0:
                    wait(dve, mixed, 1 + 16 * (b - 1) + 4 * (t - 1))
                nc.vector.tensor_tensor(
                    prod[:, t % 2, 4 * half:4 * half + 4, :],
                    desk_bank[DESK[name]][:, :].rearrange("p (e d) -> p e d", e=4),
                    combine_w[:, t, 4 * half:4 * half + 4].unsqueeze(2).to_broadcast([P, 4, P]),
                    ALU.mult).then_inc(emptied[DESK[name]], 1)

            WEIGH = [name for _, name, _ in TASKS if name[0] == "e"]

            def body(b, par, inner):
                A, F, T = parts_of(b, inner)

                def step(n, instruction):
                    instruction.then_inc(gate, 1)

                def after(n):
                    wait(dve, gate, GATE_STEPS * (b - 1) + n)

                def wide(v):
                    return v.unsqueeze(2).to_broadcast([P, QT, TOPW])

                V = nc.vector
                if not inner and b == 0:
                    dve.wait_ge(pool_setup, POOL_SETUP)
                    dve.wait_ge(x_loaded, 16 * (B - 1))
                for s in range(SLOTS):
                    if s == DVE_AT["aggr"] and F:
                        wait(dve, ln1, 3 * (b + 1) + 1)
                    if s == DVE_AT["aggr2"] and T:
                        wait(dve, ln2, 3 * (b - 1) + 1)
                    if (A if s < 32 else F):
                        u = SLOTS * b + s + 32
                        g, t, c = (s // 16 + 2) % 4, s % 16 // 4, s % 4
                        wait(dve, s_filled, u + 1)
                        V.reduce_max(neg_max[:, g % 2, t, c:c + 1], s_bank[s % 3][:, :], AX_X,
                                     negate=True).then_inc(max_done, 1)
                    if s == DVE_AT["stats"] and F:
                        for t in range(QT):
                            last = V.bn_stats(stats[:, t, :], x_all[:, bass.ts((b + 1) * QT + t, 1), :]
                                              .rearrange("p a d -> p (a d)"))
                        last.then_inc(ln1, 1)
                    if s == DVE_AT["aggr"] and F:
                        for t in range(QT):
                            last = V.bn_aggr(mean_var[:, t, :], stats[:, t, :])
                        last.then_inc(ln1, 1)
                    if s == DVE_AT["var"] and F:
                        wait(dve, ln1, 3 * (b + 1) + 2)
                        V.tensor_scalar(var_eps[:, :], mean_var[:, :, 1], EPS, None, ALU.add).then_inc(ln1, 1)
                    if s == DVE_AT["var"] and not inner and b == -1:
                        clear_rows(V, 0)
                    if s == DVE_AT["ctx3"] and T:
                        norm_ctx(b - 1, 3, b, inner)
                    if s == DVE_AT["v"] and F:
                        wait_filled(dve, b, "v", inner)
                        V.scalar_tensor_tensor(
                            out=v_ones[1 - par][:, :, :, 0:HD].rearrange("p t h d -> p (t h) d"),
                            in0=desk_bank[DESK["v"]][:, :].rearrange("p (a d) -> p a d", d=HD),
                            scalar=scales[:, 2:3], in1=b_v_all.rearrange("p (a d) -> p a d", d=HD),
                            op0=ALU.mult, op1=ALU.add).then_inc(emptied[DESK["v"]], 1)
                    if s == DVE_AT["proj"] and T:
                        wait_filled(dve, b, "proj", inner)
                        wait(dve, xb_ready, b)
                        wait(dve, mixed, 1 + 16 * (b - 1))
                        V.scalar_tensor_tensor(
                            out=x1[:, :, :].rearrange("p t d -> p (t d)"), in0=desk_bank[DESK["proj"]][:, :],
                            scalar=scales[:, 3:4], in1=x_bias[:, :, :].rearrange("p t d -> p (t d)"),
                            op0=ALU.mult, op1=ALU.add).then_inc(emptied[DESK["proj"]], 1)
                    if s == DVE_AT["stats2"] and T:
                        wait_emptied(dve, b, "proj", inner)
                        for t in range(QT):
                            last = V.bn_stats(stats2[:, t, :], x1[:, t, :])
                        last.then_inc(ln2, 1)
                    if s == DVE_AT["aggr2"] and T:
                        for t in range(QT):
                            last = V.bn_aggr(mean_var2[:, t, :], stats2[:, t, :])
                        last.then_inc(ln2, 1)
                    if s == DVE_AT["var2"] and T:
                        wait(dve, ln2, 3 * (b - 1) + 2)
                        V.tensor_scalar(var_eps2[:, :], mean_var2[:, :, 1], EPS, None, ALU.add).then_inc(ln2, 1)
                    if s == DVE_AT["ctx0"] and A:
                        norm_ctx(b, 0, b, inner)
                    if s == DVE_AT["logits"] and T:
                        wait_filled(dve, b, "logits", inner)
                        V.tensor_tensor(logits[:, :, :],
                                        desk_bank[DESK["logits"]][:, 0:QT * TOPW].rearrange("p (t e) -> p t e", e=TOPW),
                                        gate_b_all.unsqueeze(1).to_broadcast([P, QT, TOPW]),
                                        ALU.add).then_inc(emptied[DESK["logits"]], 1)
                    if s == DVE_AT["gate1"] and T:
                        wait_emptied(dve, b, "logits", inner)
                        step(1, V.reduce_max(g4[:, 0, :], logits[:, :, :], AX_X, negate=True))
                        after(1)
                        step(2, V.tensor_tensor(g10[:, 0, :, :], logits[:, :, :], wide(g4[:, 0, :]), ALU.add))
                    if s == DVE_AT["gate3"] and T:
                        wait(dve, gate_exp, b)
                        step(3, V.reduce_sum(g4[:, 1, :], g10[:, 1, :, :], AX_X))
                        after(3)
                        step(4, V.reciprocal(g4[:, 2, :], g4[:, 1, :]))
                    if s == DVE_AT["gate5"] and T:
                        after(4)
                        step(5, V.tensor_tensor(g10[:, 2, :, :], g10[:, 1, :, :], wide(g4[:, 2, :]), ALU.mult))
                        after(5)
                        step(6, V.reduce_max(g4[:, 3, :], g10[:, 2, :, :], AX_X))
                    if s == DVE_AT["gate7"] and T:
                        after(6)
                        step(7, V.tensor_tensor(g10[:, 3, :, :], g10[:, 2, :, :], wide(g4[:, 3, :]), ALU.subtract))
                        after(7)
                        step(8, V.scalar_tensor_tensor(out=g10[:, 4, :, :], in0=g10[:, 3, :, :], scalar=0.0,
                                                       in1=order[:, :, :], op0=ALU.is_ge, op1=ALU.mult))
                    if s == DVE_AT["gate9"] and T:
                        after(8)
                        step(9, V.reduce_max(g4[:, 4, :], g10[:, 4, :, :], AX_X))
                        after(9)
                        step(10, V.tensor_tensor(g10[:, 5, :, :], g10[:, 4, :, :], wide(g4[:, 4, :]), ALU.is_equal))
                    if s == DVE_AT["gate11"] and T:
                        after(10)
                        step(11, V.scalar_tensor_tensor(out=g10[:, 6, :, :], in0=g10[:, 5, :, :], scalar=-2.0,
                                                        in1=g10[:, 2, :, :], op0=ALU.mult, op1=ALU.add))
                        after(11)
                        step(12, V.reduce_max(g4[:, 5, :], g10[:, 6, :, :], AX_X))
                    if s == DVE_AT["ctx1"] and A:
                        norm_ctx(b, 1, b, inner)
                    if s == DVE_AT["gate13"] and T:
                        after(12)
                        step(13, V.tensor_tensor(g10[:, 7, :, :], g10[:, 6, :, :], wide(g4[:, 5, :]), ALU.subtract))
                        after(13)
                        step(14, V.scalar_tensor_tensor(out=g10[:, 8, :, :], in0=g10[:, 7, :, :], scalar=0.0,
                                                        in1=order[:, :, :], op0=ALU.is_ge, op1=ALU.mult))
                    if s == DVE_AT["gate15"] and T:
                        after(14)
                        step(15, V.reduce_max(g4[:, 6, :], g10[:, 8, :, :], AX_X))
                        after(15)
                        step(16, V.tensor_tensor(g10[:, 9, :, :], g10[:, 8, :, :], wide(g4[:, 6, :]), ALU.is_equal))
                        after(16)
                        step(17, V.tensor_tensor(chosen[:, :, :], g10[:, 5, :, 0:NE], g10[:, 9, :, 0:NE], ALU.add))
                    if s == DVE_AT["gate18"] and T:
                        after(17)
                        step(18, V.tensor_tensor(true_w[:, :, :], g10[:, 2, :, 0:NE], chosen[:, :, :], ALU.mult))
                        after(18)
                        step(19, V.reduce_sum(g4[:, 7, :], true_w[:, :, :], AX_X))
                        after(19)
                        step(20, V.scalar_tensor_tensor(out=g4[:, 8, :], in0=g4[:, 7, :], scalar=0.0,
                                                        in1=g4[:, 7, :], op0=ALU.is_le, op1=ALU.add))
                    if s == DVE_AT["gate21"] and T:
                        after(20)
                        step(21, V.reciprocal(g4[:, 9, :], g4[:, 8, :]))
                        after(21)
                        step(22, V.tensor_tensor(combine_w[:, :, :], true_w[:, :, :],
                                                 g4[:, 9, :].unsqueeze(2).to_broadcast([P, QT, NE]), ALU.mult))
                    if s == DVE_AT["e0a"] and T:
                        after(22)
                    for name in WEIGH:
                        if s == DVE_AT[name] and T:
                            weigh(b, name, inner)
                    if s == DVE_AT["ctx2"] and A:
                        norm_ctx(b, 2, b, inner)

            bodies(dve, body)

        @block.tensor
        def _(pe):
            T_ = nc.tensor
            pe.wait_ge(pool_setup, POOL_SETUP)
            pe.wait_ge(w_loaded, W_DMAS * 16)
            pe.wait_ge(dve_setup, DVE_SETUP)

            def scores_t(b, s, par):
                g, t, c = s // 16, s % 16 // 4, s % 4
                if s % 16 == 0:
                    wait(pe, rows_max, 16 * (4 * b + g + 1))
                wait(pe, exp_done, SLOTS * b + s - 1)
                T_.matmul(st_bank[s % 2][:, :], k_rows[par][:, 4 * g + c, P * t:P * t + P], q_rows[par][:, 4 * g + c, :],
                          start=True, stop=True).then_inc(st_filled, 1)

            def scores(b, s, par):
                u = SLOTS * b + s + 32
                g, t, c = (s // 16 + 2) % 4, s % 16 // 4, s % 4
                if s == 32:
                    wait(pe, rows_qk, 16 * LOADS * (b + 2))
                wait(pe, max_done, u if s == 0 else u - 2)
                T_.matmul(s_bank[s % 3][:, :], q_rows[par][0:ROW_MAX, 4 * g + c, P * t:P * t + P],
                          k_rows[par][0:ROW_MAX, 4 * g + c, :],
                          start=True, stop=True).then_inc(s_filled, 1)

            def values(b, n, par):
                g, t = n // 4, n % 4
                wait(pe, exp_done, SLOTS * b + 4 * n + 4)
                if t == 0:
                    wait(pe, pv_taken, 4 * b + g)
                for c in range(4):
                    last = T_.matmul(pv_bank[32 * c:32 * c + 32, :], v_ones[par][:, t, 4 * g + c, :],
                                     probs[:, 4 * (n % 2) + c, :], start=t == 0, stop=t == QT - 1)
                last.then_inc(pv_done, 1)

            def task(b, name, par, inner):
                desk, bank = DESK[name], desk_bank[DESK[name]]
                wait(pe, emptied[desk], place(b, name, inner))
                if name.startswith("rows"):
                    g = int(name[-1])
                    n = 4 * (b + (g == 0)) + g
                    wait(pe, max_split, 4 * n + 4)
                    rows = bank[0:12, 0:S // 2].bitcast(BF16)
                    for t in range(QT):
                        last = T_.transpose(rows[:, P * t:P * t + P], max_parts[:, g % 2, t, :], identity_bf[:, :])
                elif name == "xn_t":
                    wait(pe, xn_ready, b + 2)
                    for t in range(QT):
                        last = T_.transpose(bank[:, P * t:P * t + P], xn[:, t, :], identity[:, :])
                elif name in "qk":
                    wait_emptied(pe, b, "xn_t", inner)
                    last = T_.matmul(bank[:, :], w_qk_t[:, "qk".index(name), :], xn_t[:, :], start=True, stop=True)
                elif name == "v":
                    for t in range(QT):
                        last = T_.matmul(bank[:, P * t:P * t + P], xn_t[:, P * t:P * t + P], w_v_t,
                                         start=True, stop=True)
                elif name in ("ctx0", "ctx1", "ctx2", "ctx3"):
                    g = int(name[-1])
                    wait(pe, pv_taken, 4 * (b - (g == 3)) + g + 1)
                    for t in range(QT):
                        last = T_.transpose(bank[:, P * t:P * t + P], ctx_raw[:, g % 2, P * t:P * t + P],
                                            identity[:, :])
                elif name == "ctx_t":
                    wait_emptied(pe, b, "ctx3", inner)
                    for t in range(QT):
                        last = T_.transpose(bank[:, P * t:P * t + P], ctx_tok[:, t, :], identity[:, :])
                elif name == "proj":
                    wait_emptied(pe, b, "ctx_t", inner)
                    for t in range(QT):
                        last = T_.matmul(bank[:, P * t:P * t + P], ctx_t[:, P * t:P * t + P], w_o_t,
                                         start=True, stop=True)
                elif name == "xn2_t":
                    wait(pe, xn2_ready, b)
                    for t in range(QT):
                        last = T_.transpose(bank[:, P * t:P * t + P], xn2[:, t, :], identity[:, :])
                elif name == "logits":
                    wait_emptied(pe, b, "xn2_t", inner)
                    for t in range(QT):
                        last = T_.matmul(bank[:, TOPW * t:TOPW * t + TOPW], xn2_t[:, P * t:P * t + P], gate_t,
                                         start=True, stop=True)
                else:
                    t, half = int(name[1]), "ab".index(name[2])
                    T_.matmul(bank[:, :], xn2_t[:, P * t:P * t + P],
                              w_exp[:, 512 * half:512 * half + 512], start=True, stop=False)
                    last = T_.matmul(bank[:, :], ones3[:, :], eb_rows[:, 512 * half:512 * half + 512],
                                     start=False, stop=True)
                last.then_inc(filled[desk], 1)

            def body(b, par, inner):
                here = dict(zip("AFT", parts_of(b, inner)))
                if not inner and b == 0:
                    pe.wait_ge(eb_loaded, 16)
                for s in range(SLOTS):
                    if here["A"]:
                        scores_t(b, s, par)
                    if s < 32 and here["A"]:
                        scores(b, s, par)
                    if s >= 32 and here["F"]:
                        scores(b, s, 1 - par)
                    if s % 4 == PV_PHASE:
                        if s > 3 and here["A"]:
                            values(b, s // 4 - 1, par)
                        if s < 4 and here["T"]:
                            values(b - 1, 15, 1 - par)
                    if s in PE_SLOT and here[WHO[PE_SLOT[s]]]:
                        task(b, PE_SLOT[s], par, inner)

            bodies(pe, body)


def kernel(**inputs):
    import concourse.bacc as _bacc
    from concourse.bass_utils import run_bass_kernel_spmd as _run

    a = {name[3:]: np.asarray(v) for name, v in inputs.items()}
    qk_order = np.arange(P).reshape(HEADS, HD).T.ravel()
    weights = np.concatenate([a["attn_w_q"].T[:, qk_order], a["attn_w_k"].T[:, qk_order], a["attn_w_v"].T,
                              a["attn_w_o"].T, a["ffn_gate_w"].T], axis=1)
    scalars = [a[f"attn_s_{n}"].reshape(1) for n in "qkvo"]
    arrays = {
        "x": a["attn_x"],
        "weights": weights,
        "experts": a["ffn_expert_w"].transpose(1, 0, 2).reshape(P, NE * P),
        "vectors": np.concatenate([np.tile(a["attn_b_v"], 4), a["attn_b_o"], a["ffn_gate_b"]] + scalars),
        "qk_biases": np.stack([a["attn_b_q"][qk_order], a["attn_b_k"][qk_order]], axis=1),
        "expert_b": a["ffn_expert_b"],
    }
    arrays = {name: np.ascontiguousarray(v) for name, v in arrays.items()}
    nc = _bacc.Bacc("TRN2", target_bir_lowering=False, num_devices=1)
    args = [nc.dram_tensor(name, v.shape, mybir.dt.from_np(v.dtype), kind="ExternalInput").ap()
            for name, v in arrays.items()]
    args.append(nc.dram_tensor("layer_out", arrays["x"].shape, F32, kind="ExternalOutput").ap())
    build(nc, *args)
    return _run(nc, [arrays], core_ids=[0]).results[0]["layer_out"]
```

```python
from contextlib import ExitStack

import numpy as np

import concourse.bass as bass
from concourse import mybir

F32 = mybir.dt.float32
BF16 = mybir.dt.bfloat16
ALU = mybir.AluOpType
ACT = mybir.ActivationFunctionType
AX_X = mybir.AxisListType.X

P = 128
EPS = 1e-5
HEADS, HD = 16, 8
TOPW = 10
NE = 8
ROW_MAX = P - 3
SLOTS = 64
LEAD = 31
FIRST_TILES = 29
CATCH_UP = 2
PV_PHASE = 1
WARM_FIRST, WARM_LAST = 40, 14
GATE_STEPS = 22
W_DMAS = 5
POOL_SETUP = 6
LOADS = 12

BF16_ONES = float(np.array([0x3F803F80], np.uint32).view(np.float32)[0])

Q_TERMS = (0, 0, 0, 1, 1, 2)
K_TERMS = (0, 1, 2, 0, 1, 0)

TASKS = (
    (6, "ctx3", "T"), (7, "rows1", "A"), (9, "xn_t", "F"), (11, "ctx_t", "T"), (12, "q", "F"),
    (14, "proj", "T"), (15, "k", "F"), (19, "v", "F"), (20, "rows2", "A"), (23, "ctx0", "A"),
    (27, "xn2_t", "T"), (31, "logits", "T"), (35, "ctx1", "A"), (36, "rows3", "A"), (39, "e0a", "T"),
    (43, "e0b", "T"), (47, "e1a", "T"), (50, "e1b", "T"), (51, "e2a", "T"), (52, "e2b", "T"),
    (54, "rows0", "F"), (55, "ctx2", "A"), (59, "e3a", "T"), (63, "e3b", "T"),
)
ACT_AT = {"pv3": 3, "rows1": 7, "xn_t": 9, "ctx_t": 12, "q": 13, "k": 17, "pv0": 19, "rows2": 23, "xn2_t": 28,
          "gate": 31, "pv1": 33, "rows3": 37, "e1a": 48, "e1b": 50, "pv2": 51, "rows0": 57}
DVE_AT = {"stats": 1, "aggr": 2, "var": 2, "ctx3": 6, "proj": 14, "stats2": 16, "v": 19, "aggr2": 21, "var2": 21,
          "ctx0": 27, "logits": 31, "gate1": 31, "gate3": 32, "gate5": 33, "gate7": 35, "ctx1": 35, "gate9": 36,
          "gate11": 37, "gate13": 39, "gate15": 40, "gate18": 42, "gate21": 44, "e0a": 44, "e0b": 45, "e2a": 52,
          "e2b": 52, "ctx2": 59, "e3a": 61, "e3b": 63}
POOL_ORDER = ("split1", "norm", "x_bias", "q", "split2", "k", "norm2", "split3", "split0", "mix0", "mix1", "mix2",
              "mix3")
WEIGH = [name for _, name, _ in TASKS if name[0] == "e"]
DESK = {name: n % 2 for n, (_, name, _) in enumerate(TASKS)}
PE_SLOT = {slot: name for slot, name, _ in TASKS}
WHO = {name: who for _, name, who in TASKS}


W_QK, W_V, W_O, W_GATE, W_END = 0, 2 * P, 3 * P, 4 * P, 4 * P + TOPW
V_BV, V_BO, V_BG, V_SCALES, V_END = 0, 4 * P, 5 * P, 5 * P + TOPW, 5 * P + TOPW + 4


def build(nc, x, weights, experts, vectors, qk_biases, expert_b, out):
    B, S, D = x.shape
    QT = S // P
    assert D == P and S == 512 and HEADS * HD == D and experts.shape[1] == NE * D

    def present(b):
        return {"A": 0 <= b < B, "F": b + 1 < B, "T": b >= 1}

    def uses(b, desk):
        return sum(present(b)[who] for _, name, who in TASKS if DESK[name] == desk)

    def place(b, name, inner):
        desk = DESK[name]
        first = 1 if inner else b
        here = present(first)
        n = sum(uses(bb, desk) for bb in range(-1, first))
        for _, other, who in TASKS:
            if other == name:
                break
            n += here[who] and DESK[other] == desk
        return n + (b - 1) * uses(1, desk) if inner else n

    def scores_in(b, s, inner):
        if inner or b > 0:
            return [(b, s)]
        if b < 0:
            return [(b, s)] if SLOTS - LEAD <= s < SLOTS - LEAD + FIRST_TILES else []
        tiles = range(min(FIRST_TILES + CATCH_UP * s, s + LEAD), min(FIRST_TILES + CATCH_UP * (s + 1), s + LEAD + 1))
        return [(b, u - LEAD) if u >= LEAD else (-1, SLOTS + u - LEAD) for u in tiles]

    def s_bank_of(s):
        return 1 if s == SLOTS - 1 else s % 3

    ctx = ExitStack()
    with ctx:
        def sb(name, shape, dt=F32):
            return ctx.enter_context(nc.sbuf_tensor(name, shape, dt))

        def ps(name):
            return ctx.enter_context(nc.psum_tensor(name, [P, 512], F32))

        def sem(name):
            return ctx.enter_context(nc.semaphore(name))

        st_bank = [ps(f"st_bank{i}") for i in range(2)]
        s_bank = [ps(f"s_bank{i}") for i in range(3)]
        pv_bank = ps("pv_bank")
        desk_bank = [ps(f"desk_bank{i}") for i in range(2)]

        identity = sb("identity", [P, P])
        identity_bf = sb("identity_bf", [P, P], BF16)
        w_all = sb("w_all", [P, W_END])
        w_qk_t = w_all[:, W_QK:W_V].rearrange("i (n o) -> i n o", n=2)
        w_v_t = w_all[:, W_V:W_O]
        w_o_t = w_all[:, W_O:W_GATE]
        gate_t = w_all[:, W_GATE:W_END]
        w_exp = sb("w_exp", [P, NE * P])
        vec_all = sb("vec_all", [P, V_END])
        b_v_all = vec_all[:, V_BV:V_BO]
        b_o_all = vec_all[:, V_BO:V_BG]
        gate_b_all = vec_all[:, V_BG:V_SCALES]
        scales = vec_all[:, V_SCALES:V_END]
        eb_rows = sb("eb_rows", [3, NE * P], BF16)
        ones3 = sb("ones3", [3, P], BF16)
        qk_scale = sb("qk_scale", [P, 2])
        qk_bias_nat = sb("qk_bias_nat", [P, 2])
        qk_bias = sb("qk_bias", [P, 2])
        neg_half = sb("neg_half", [P, QT])
        table_warm = sb("table_warm", [P, QT])
        zeros = sb("zeros", [P, QT, 4])
        order = sb("order", [P, QT, TOPW])

        x_all = sb("x_all", [P, B * QT, P])
        stats = sb("stats", [P, QT, 6])
        mean_var = sb("mean_var", [P, QT, 2])
        var_eps = sb("var_eps", [P, QT])
        rstd = sb("rstd", [P, QT])
        x_centred = sb("x_centred", [P, QT, P])
        xn = sb("xn", [P, QT, P])
        xn_t = sb("xn_t", [P, S])
        qk_full = sb("qk_full", [P, 2, S])
        qk_rest = sb("qk_rest", [P, 2, S])
        qk_parts = sb("qk_parts", [P, 2, 3, S], BF16)
        q_rows = [sb(f"q_rows{i}", [P, HEADS, S], BF16) for i in range(2)]
        k_rows = [sb(f"k_rows{i}", [P, HEADS, S], BF16) for i in range(2)]
        v_ones = [sb(f"v_ones{i}", [P, QT, HEADS, 32]) for i in range(2)]
        neg_max = sb("neg_max", [P, 2, QT, 4])
        neg_rest = sb("neg_rest", [P, QT, 4])
        max_parts = sb("max_parts", [P, 2, QT, 12], BF16)
        max_rows = sb("max_rows", [12, 2, S], BF16)
        probs = sb("probs", [P, 8, S])
        ctx_raw = sb("ctx_raw", [P, 2, S])
        inv_sum = sb("inv_sum", [P, QT, 4])
        ctx_tok = sb("ctx_tok", [P, QT, P])
        ctx_t = sb("ctx_t", [P, S])
        x_bias = sb("x_bias", [P, QT, P])
        x1 = sb("x1", [P, QT, P])
        stats2 = sb("stats2", [P, QT, 6])
        mean_var2 = sb("mean_var2", [P, QT, 2])
        var_eps2 = sb("var_eps2", [P, QT])
        rstd2 = sb("rstd2", [P, QT])
        x1_centred = sb("x1_centred", [P, QT, P])
        xn2 = sb("xn2", [P, QT, P])
        xn2_t = sb("xn2_t", [P, S])
        logits = sb("logits", [P, QT, TOPW])
        g4 = sb("g4", [P, 10, QT])
        g10 = sb("g10", [P, 10, QT, TOPW])
        true_w = sb("true_w", [P, QT, NE])
        chosen = sb("chosen", [P, QT, NE])
        combine_w = sb("combine_w", [P, QT, NE])
        prod = sb("prod", [P, 2, NE, P])
        eb_row = prod[0:1, 0, :, :].rearrange("p e d -> p (e d)")
        eb_rest = prod[0:1, 1, :, :].rearrange("p e d -> p (e d)")
        eb_parts = sb("eb_parts", [1, 3, NE * P], BF16)
        sum4 = sb("sum4", [P, 4, P])
        sum2 = sb("sum2", [P, 2, P])
        sum1 = sb("sum1", [P, P])
        last_sum4, last_sum2, last_sum1 = sb("last_sum4", [P, 4, P]), sb("last_sum2", [P, 2, P]), sb("last_sum1", [P, P])
        y = sb("y", [P, QT, P])

        w_loaded = sem("w_loaded")
        x0_loaded = sem("x0_loaded")
        x_loaded = sem("x_loaded")
        pool_setup = sem("pool_setup")
        scales_ready = sem("scales_ready")
        v_ones_set = sem("v_ones_set")
        eb_split = sem("eb_split")
        eb_loaded = sem("eb_loaded")
        q_cleared = [sem(f"q_cleared{i}") for i in range(2)]
        k_cleared = [sem(f"k_cleared{i}") for i in range(2)]
        filled = [sem("desk0_filled"), sem("desk1_filled")]
        emptied = [sem("desk0_emptied"), sem("desk1_emptied")]
        ln1 = sem("ln1")
        ln1_centred = sem("ln1_centred")
        dve_centred = sem("dve_centred")
        xn_ready = sem("xn_ready")
        qk_split = [sem("q_split"), sem("k_split")]
        rows_qk = sem("rows_qk")
        s_filled = sem("s_filled")
        max_done = sem("max_done")
        max_split = sem("max_split")
        rows_max = sem("rows_max")
        st_filled = sem("st_filled")
        exp_done = sem("exp_done")
        pv_done = sem("pv_done")
        pv_taken = sem("pv_taken")
        inv_done = sem("inv_done")
        xb_ready = sem("xb_ready")
        ln2 = sem("ln2")
        ln2_centred = sem("ln2_centred")
        xn2_ready = sem("xn2_ready")
        gate = sem("gate")
        gate_exp = sem("gate_exp")
        mixed = sem("mixed")
        last_mixed = sem("last_mixed")
        y_free = sem("y_free")

        block = ctx.enter_context(nc.Block())

        def wait(eng, semaphore, count):
            if not (isinstance(count, int) and count <= 0):
                eng.wait_ge(semaphore, count)

        def wait_filled(eng, b, name, inner):
            wait(eng, filled[DESK[name]], place(b, name, inner) + 1)

        def wait_emptied(eng, b, name, inner):
            wait(eng, emptied[DESK[name]], place(b, name, inner) + 1)

        def bodies(eng, body):
            body(-1, 1, False)
            body(0, 0, False)
            with eng.Fori(1, B - 2, 2) as b:
                body(b, 1, True)
                body(b + 1, 0, True)
            body(B - 1, 1, False)
            body(B, 0, False)

        def clear_q(eng, par, half):
            eng.memset(q_rows[par][:, 8 * half:8 * half + 8, :].bitcast(F32), 0.0).then_inc(q_cleared[par], 1)

        def clear_k(eng, par, half):
            eng.memset(k_rows[par][:, 8 * half:8 * half + 8, :].bitcast(F32), BF16_ONES).then_inc(k_cleared[par], 1)

        def parts_of(b, inner):
            return (True, True, True) if inner else tuple(present(b)[w] for w in "AFT")

        last_bank = dict(zip(WEIGH, st_bank + s_bank + [pv_bank] + desk_bank))

        def is_first(b, inner):
            return not inner and b == -1

        def is_last(b, inner):
            return not inner and b == B

        def per_token(v):
            return v.unsqueeze(2).to_broadcast([P, QT, P])

        def weigh(eng, b, name, inner):
            t, half = int(name[1]), "ab".index(name[2])
            wait_filled(eng, b, name, inner)
            if t == 3 and half == 0 and is_last(b, inner):
                eng.wait_ge(last_mixed, 4)
            elif t >= 2 and half == 0:
                wait(eng, mixed, 1 + 16 * (b - 1) + 4 * (t - 1))
            four = slice(NE // 2 * half, NE // 2 * (half + 1))
            bank = last_bank[name] if is_last(b, inner) else desk_bank[DESK[name]]
            return bank[:, :], combine_w[:, t, four], prod[:, t % 2, four, :]

        def split_qk(eng, b, n):
            eng.tensor_tensor(qk_parts[:, n, 1, :], qk_full[:, n, :], qk_parts[:, n, 0, :],
                              ALU.subtract).then_inc(qk_split[n], 1)
            eng.tensor_tensor(qk_rest[:, n, :], qk_full[:, n, :], qk_parts[:, n, 0, :],
                              ALU.subtract).then_inc(qk_split[n], 1)
            eng.wait_ge(qk_split[n], 3 * (b + 1) + 2)
            eng.tensor_tensor(qk_parts[:, n, 2, :], qk_rest[:, n, :], qk_parts[:, n, 1, :],
                              ALU.subtract).then_inc(qk_split[n], 1)

        def mix(eng, t, sums, steps, n):
            four, two, one = sums
            eng.tensor_tensor(four[:, :, :], prod[:, t % 2, 0:4, :], prod[:, t % 2, 4:8, :], ALU.add).then_inc(steps, 1)
            eng.wait_ge(steps, n + 1)
            eng.tensor_tensor(two[:, :, :], four[:, 0:2, :], four[:, 2:4, :], ALU.add).then_inc(steps, 1)
            eng.wait_ge(steps, n + 2)
            eng.tensor_tensor(one[:, :], two[:, 0, :], two[:, 1, :], ALU.add).then_inc(steps, 1)
            eng.wait_ge(steps, n + 3)
            eng.tensor_tensor(y[:, t, :], one[:, :], x1[:, t, :], ALU.add).then_inc(steps, 1)

        @block.sync
        def _(sync):
            x_v = x.rearrange("b (p t) d -> p b (t d)", p=P)
            out_v = out.rearrange("b (p t) d -> p b (t d)", p=P)
            sync.dma_start(x_all[:, 0:QT, :], x_v[:, 0, :]).then_inc(x0_loaded, 16)
            sync.dma_start(w_all[:, :], weights).then_inc(w_loaded, 16)
            sync.dma_start(vec_all[:, :], vectors.partition_broadcast(P)).then_inc(w_loaded, 16)
            sync.dma_start(qk_bias_nat[:, :], qk_biases).then_inc(w_loaded, 16)
            sync.dma_start(eb_row, expert_b.rearrange("(a e) h -> a (e h)", a=1)).then_inc(w_loaded, 16)
            sync.dma_start(w_exp[:, :], experts).then_inc(w_loaded, 16)
            for b in range(1, B):
                sync.dma_start(x_all[:, b * QT:(b + 1) * QT, :], x_v[:, b, :]).then_inc(x_loaded, 16)

            def put_max_rows(b, g, par, inner):
                name = f"rows{g}"
                wait_emptied(sync, b - (g == 0), name, inner)
                sync.dma_start(q_rows[par][ROW_MAX:P, 4 * g:4 * g + 4, :], max_rows[:, g % 2, :]).then_inc(rows_max, 16)

            def body(b, par, inner):
                A, F, T = parts_of(b, inner)
                if not inner and b == 0:
                    sync.wait_ge(eb_split, 4)
                    sync.dma_start(eb_rows[:, :], eb_parts[:, :, :]).then_inc(eb_loaded, 16)
                if A:
                    put_max_rows(b, 1, par, inner)
                if F:
                    for n, (rows, terms) in enumerate(((q_rows[1 - par], Q_TERMS), (k_rows[1 - par], K_TERMS))):
                        for part in range(3):
                            if part == 0:
                                if not inner:
                                    sync.wait_ge((q_cleared, k_cleared)[n][1 - par], 2)
                                wait_emptied(sync, b, "qk"[n], inner)
                            else:
                                wait(sync, qk_split[n], 3 * (b + 1) + (1, 3)[part - 1])
                            for t in (t for t in range(6) if terms[t] == part):
                                sync.dma_start(rows[HD * t:HD * t + HD, :, :], qk_parts[:, n, part, :])\
                                    .then_inc(rows_qk, 16)
                if A:
                    put_max_rows(b, 2, par, inner)
                    put_max_rows(b, 3, par, inner)
                if F:
                    put_max_rows(b + 1, 0, 1 - par, inner)
                if T:
                    if is_last(b, inner):
                        sync.wait_ge(last_mixed, 8)
                        sync.wait_ge(mixed, 1 + 16 * (B - 1) + 8)
                    else:
                        wait(sync, mixed, 1 + 16 * b)
                    sync.dma_start(out_v[:, bass.ds(b - 1, 1), :], y[:, :, :].rearrange("p (a t) d -> p a (t d)", a=1))\
                        .then_inc(y_free, 16)

            bodies(sync, body)
            sync.wait_ge(y_free, 16 * (B + 1))

        @block.gpsimd
        def _(pool):
            pool.memset(identity[:, :], 0.0).then_inc(pool_setup, 1)
            pool.wait_ge(pool_setup, 1)
            pool.affine_select(out=identity[:, :], in_=identity[:, :], compare_op=ALU.not_equal, fill=1.0,
                               base=0, pattern=[[-1, P]], channel_multiplier=1).then_inc(pool_setup, 1)
            pool.wait_ge(pool_setup, 2)
            pool.tensor_copy(identity_bf[:, :], identity[:, :]).then_inc(pool_setup, 1)
            pool.memset(ones3[:, :], 1.0).then_inc(pool_setup, 1)
            for n in range(TOPW):
                last = pool.memset(order[:, :, n:n + 1], float(TOPW - n))
            last.then_inc(pool_setup, 1)
            pool.memset(zeros[:, :, :], 0.0)
            pool.memset(neg_half[:, :], -0.5).then_inc(pool_setup, 1)
            pool.wait_ge(pool_setup, POOL_SETUP)

            def split_biases():
                pool.wait_ge(w_loaded, W_DMAS * 16)
                pool.tensor_copy(eb_parts[:, 0, :], eb_row).then_inc(eb_split, 1)
                pool.wait_ge(eb_split, 1)
                pool.tensor_tensor(eb_parts[:, 1, :], eb_row, eb_parts[:, 0, :], ALU.subtract).then_inc(eb_split, 1)
                pool.tensor_tensor(eb_rest, eb_row, eb_parts[:, 0, :], ALU.subtract).then_inc(eb_split, 1)
                pool.wait_ge(eb_split, 3)
                pool.tensor_tensor(eb_parts[:, 2, :], eb_rest, eb_parts[:, 1, :], ALU.subtract).then_inc(eb_split, 1)

            def split_max(b, g):
                n = 4 * b + g
                r = g % 2
                whole = neg_max[:, r, :, :]

                def part(k):
                    return max_parts[:, r, :, 4 * k:4 * k + 4]
                wait(pool, max_done, 16 * (n + 1))
                pool.tensor_tensor(part(0), whole, zeros[:, :, :], ALU.add).then_inc(max_split, 1)
                pool.wait_ge(max_split, 4 * n + 1)
                pool.tensor_tensor(part(1), whole, part(0), ALU.subtract).then_inc(max_split, 1)
                pool.tensor_tensor(neg_rest[:, :, :], whole, part(0), ALU.subtract).then_inc(max_split, 1)
                pool.wait_ge(max_split, 4 * n + 3)
                pool.tensor_tensor(part(2), neg_rest[:, :, :], part(1), ALU.subtract).then_inc(max_split, 1)

            def body(b, par, inner):
                A, F, T = parts_of(b, inner)
                if not inner and b == 0:
                    pool.wait_ge(x_loaded, 16 * (B - 1))
                for name in POOL_ORDER:
                    if name == "split1" and A:
                        split_max(b, 1)
                    if name == "norm" and is_first(b, inner):
                        pool.wait_ge(ln1, 3)
                        pool.tensor_tensor(rstd[:, :], var_eps[:, :], neg_half[:, :], ALU.pow)\
                            .then_inc(ln1_centred, 2)
                        clear_q(pool, 0, 0)
                        clear_q(pool, 0, 1)
                    elif name == "norm" and F:
                        wait(pool, ln1, 3 * (b + 1) + 2)
                        pool.tensor_tensor(x_centred[:, :, :], x_all[:, bass.ts(b + 1, QT), :],
                                           per_token(mean_var[:, :, 0]), ALU.subtract).then_inc(ln1_centred, 1)
                        wait(pool, ln1, 3 * (b + 1) + 3)
                        pool.tensor_tensor(rstd[:, :], var_eps[:, :], neg_half[:, :], ALU.pow)\
                            .then_inc(ln1_centred, 1)
                        wait(pool, ln1_centred, 2 * (b + 2))
                        pool.tensor_tensor(xn[:, :, :], x_centred[:, :, :], per_token(rstd[:, :]), ALU.mult)\
                            .then_inc(xn_ready, 1)
                    if name == "x_bias" and T:
                        pool.tensor_tensor(x_bias[:, :, :], x_all[:, bass.ts(b - 1, QT), :],
                                           b_o_all.unsqueeze(1).to_broadcast([P, QT, P]), ALU.add)\
                            .then_inc(xb_ready, 1)
                    if name in ("q", "k") and F:
                        n = "qk".index(name)
                        if inner or b > -1 or name == "q":
                            wait_emptied(pool, b, name, inner)
                            split_qk(pool, b, n)
                        if name == "k" and not inner and b == -1:
                            for half in range(2):
                                clear_q(pool, 1, half)
                                clear_k(pool, 1, half)
                            split_biases()
                    if name == "split2" and A:
                        split_max(b, 2)
                    if name == "norm2" and is_last(b, inner):
                        pool.wait_ge(ln2, 3 * B)
                        pool.tensor_tensor(rstd2[:, :], var_eps2[:, :], neg_half[:, :], ALU.pow)\
                            .then_inc(ln2_centred, 2)
                    elif name == "norm2" and T:
                        wait(pool, ln2, 3 * (b - 1) + 2)
                        pool.tensor_tensor(x1_centred[:, :, :], x1[:, :, :],
                                           per_token(mean_var2[:, :, 0]), ALU.subtract).then_inc(ln2_centred, 1)
                        wait(pool, ln2, 3 * (b - 1) + 3)
                        pool.tensor_tensor(rstd2[:, :], var_eps2[:, :], neg_half[:, :], ALU.pow)\
                            .then_inc(ln2_centred, 1)
                        wait(pool, ln2_centred, 2 * b)
                        pool.tensor_tensor(xn2[:, :, :], x1_centred[:, :, :], per_token(rstd2[:, :]), ALU.mult)\
                            .then_inc(xn2_ready, 1)
                    if name == "split3" and A:
                        split_max(b, 3)
                    if name == "split0" and F:
                        split_max(b + 1, 0)
                    if name.startswith("mix") and T:
                        t = int(name[-1])
                        tile = t // 2 if is_last(b, inner) else t
                        if tile == t or t == 2:
                            wait_emptied(pool, b, f"e{t}b", inner)
                            if t == 0:
                                wait(pool, y_free, 16 * b)
                            mix(pool, t, (sum4, sum2, sum1), mixed, 1 + 16 * (b - 1) + 4 * tile)

            pool.memset(sum1[:, :], 0.0).then_inc(mixed, 1)
            pool.memset(y[:, :, :], 0.0).then_inc(y_free, 16)
            pool.wait_ge(x0_loaded, 16)
            bodies(pool, body)

        @block.scalar
        def _(act):
            def take_pv(b, g):
                n = 4 * b + g
                wait(act, pv_done, 4 * n + 4)
                act.copy(ctx_raw[:, g % 2, :], pv_bank[:, :]).then_inc(pv_taken, 1)

            def take_rows(b, name, inner):
                g = int(name[-1])
                wait_filled(act, b, name, inner)
                act.copy(max_rows[:, g % 2, :], desk_bank[DESK[name]][0:12, 0:S // 2].bitcast(BF16))\
                    .then_inc(emptied[DESK[name]], 1)

            def take(b, name, dst, inner):
                wait_filled(act, b, name, inner)
                act.copy(dst[:, :], desk_bank[DESK[name]][:, :]).then_inc(emptied[DESK[name]], 1)

            def body(b, par, inner):
                A, F, T = parts_of(b, inner)
                waited = False
                for s in range(SLOTS):
                    if A:
                        a = SLOTS * b + s
                        wait(act, st_filled, a + 1)
                        if s % 4 == 0:
                            wait(act, pv_done, 16 * b + s // 4 - 1)
                        act.activation(probs[:, s % 8, :], st_bank[s % 2][:, :], ACT.Exp).then_inc(exp_done, 1)
                    if s == ACT_AT["pv3"] and T:
                        take_pv(b - 1, 3)
                    if s == ACT_AT["rows1"] and A:
                        take_rows(b, "rows1", inner)
                    if s == ACT_AT["xn_t"] and F:
                        take(b, "xn_t", xn_t, inner)
                    if s in (ACT_AT["q"], ACT_AT["k"]) and F:
                        n, name = (0, "q") if s == ACT_AT["q"] else (1, "k")
                        bank = desk_bank[DESK[name]]
                        if not inner and b == -1:
                            act.wait_ge(scales_ready, 1)
                        wait_filled(act, b, name, inner)
                        act.activation(qk_parts[:, n, 0, :], bank[:, :], ACT.Identity,
                                       scale=qk_scale[:, n:n + 1], bias=qk_bias[:, n:n + 1])
                        act.activation(qk_full[:, n, :], bank[:, :], ACT.Identity,
                                       scale=qk_scale[:, n:n + 1], bias=qk_bias[:, n:n + 1])\
                            .then_inc(emptied[DESK[name]], 1)
                    if s == ACT_AT["ctx_t"] and T:
                        take(b, "ctx_t", ctx_t, inner)
                    if s == ACT_AT["pv0"] and A:
                        take_pv(b, 0)
                    if s == ACT_AT["rows2"] and A:
                        take_rows(b, "rows2", inner)
                    if s == ACT_AT["xn2_t"] and T:
                        take(b, "xn2_t", xn2_t, inner)
                    if s == ACT_AT["gate"] and T:
                        wait(act, gate, GATE_STEPS * (b - 1) + 2)
                        act.activation(g10[:, 1, :, :], g10[:, 0, :, :], ACT.Exp).then_inc(gate_exp, 1)
                    if s == ACT_AT["pv1"] and A:
                        take_pv(b, 1)
                    if s == ACT_AT["rows3"] and A:
                        take_rows(b, "rows3", inner)
                    if s == ACT_AT["pv2"] and A:
                        take_pv(b, 2)
                    if s == ACT_AT["rows0"] and F:
                        take_rows(b, "rows0", inner)
                    for name in WEIGH:
                        if s == ACT_AT.get(name) and T and not is_last(b, inner):
                            if not waited:
                                wait(act, gate, GATE_STEPS * b)
                                waited = True
                            desk, w, result = weigh(act, b, name, inner)
                            for e in range(NE // 2):
                                last = act.activation(result[:, e, :], desk[:, P * e:P * e + P], ACT.Copy,
                                                      scale=w[:, e:e + 1])
                            last.then_inc(emptied[DESK[name]], 1)

            act.wait_ge(pool_setup, POOL_SETUP)
            act.activation(table_warm[:, :], neg_half[:, :], ACT.Exp)
            bodies(act, body)

        @block.vector
        def _(dve):
            def set_up():
                dve.wait_ge(w_loaded, W_DMAS * 16)
                root = float(1.0 / np.sqrt(np.float32(HD)))
                nc.vector.tensor_scalar(qk_scale[:, 0:1], scales[:, 0:1], root, None, ALU.mult)
                nc.vector.tensor_copy(qk_scale[:, 1:2], scales[:, 1:2])
                nc.vector.tensor_scalar(qk_bias[:, 0:1], qk_bias_nat[:, 0:1], root, None, ALU.mult)
                nc.vector.tensor_copy(qk_bias[:, 1:2], qk_bias_nat[:, 1:2]).then_inc(scales_ready, 1)
                clear_k(nc.vector, 0, 1)
                for i in range(2):
                    nc.vector.memset(v_ones[i][:, :, :, HD + 1:32], 0.0)
                    last = nc.vector.memset(v_ones[i][:, :, :, HD:HD + 1], 1.0)
                last.then_inc(v_ones_set, 1)

            def norm_ctx(b, g, body_b, inner):
                n, name = 4 * b + g, f"ctx{g}"
                wait_filled(dve, body_b, name, inner)
                bank = desk_bank[DESK[name]][:, :].rearrange("p (t c k) -> p t c k", t=QT, k=32)
                nc.vector.reciprocal(inv_sum[:, :, :], bank[:, :, :, HD]).then_inc(inv_done, 1)
                wait(dve, inv_done, n + 1)
                nc.vector.tensor_tensor(
                    ctx_tok[:, :, 32 * g:32 * g + 32].rearrange("p t (c d) -> p t c d", d=HD),
                    bank[:, :, :, 0:HD], inv_sum[:, :, :].unsqueeze(3).to_broadcast([P, QT, 4, HD]),
                    ALU.mult).then_inc(emptied[DESK[name]], 1)

            def weigh_here(b, name, inner):
                desk, w, result = weigh(dve, b, name, inner)
                nc.vector.tensor_tensor(result, desk.rearrange("p (e d) -> p e d", e=NE // 2),
                                        w.unsqueeze(2).to_broadcast([P, NE // 2, P]), ALU.mult)\
                    .then_inc(emptied[DESK[name]], 1)

            def body(b, par, inner):
                A, F, T = parts_of(b, inner)

                def step(n, instruction):
                    instruction.then_inc(gate, 1)

                def after(n):
                    wait(dve, gate, GATE_STEPS * (b - 1) + n)

                def wide(v):
                    return v.unsqueeze(2).to_broadcast([P, QT, TOPW])

                V = nc.vector
                if not inner and b == 0:
                    dve.wait_ge(pool_setup, POOL_SETUP)
                    dve.wait_ge(x_loaded, 16 * (B - 1))
                for s in range(SLOTS):
                    if s == DVE_AT["aggr"] and F:
                        wait(dve, ln1, 3 * (b + 1) + 1)
                    if s == DVE_AT["aggr2"] and T:
                        wait(dve, ln2, 3 * (b - 1) + 1)
                    for own_b, own_s in scores_in(b, s, inner):
                        if A if own_s < SLOTS - LEAD else F:
                            u = SLOTS * own_b + own_s + LEAD
                            of = (own_s + LEAD) % SLOTS
                            g, t, c = of // 16, of % 16 // 4, of % 4
                            wait(dve, s_filled, u + 1)
                            V.reduce_max(neg_max[:, g % 2, t, c:c + 1], s_bank[s_bank_of(own_s)][:, :], AX_X,
                                         negate=True).then_inc(max_done, 1)
                    if s == DVE_AT["stats"] and F:
                        for t in range(QT):
                            last = V.bn_stats(stats[:, t, :], x_all[:, bass.ts((b + 1) * QT + t, 1), :]
                                              .rearrange("p a d -> p (a d)"))
                        last.then_inc(ln1, 1)
                    if s == DVE_AT["aggr"] and F:
                        for t in range(QT):
                            last = V.bn_aggr(mean_var[:, t, :], stats[:, t, :])
                        last.then_inc(ln1, 1)
                    if s == DVE_AT["var"] and F:
                        wait(dve, ln1, 3 * (b + 1) + 2)
                        V.tensor_scalar(var_eps[:, :], mean_var[:, :, 1], EPS, None, ALU.add).then_inc(ln1, 1)
                    if s == DVE_AT["var"] and not inner and b == -1:
                        V.tensor_tensor(x_centred[:, :, :], x_all[:, 0:QT, :], per_token(mean_var[:, :, 0]),
                                        ALU.subtract).then_inc(dve_centred, 1)
                        dve.wait_ge(dve_centred, 1)
                        dve.wait_ge(ln1_centred, 2)
                        V.tensor_tensor(xn[:, :, :], x_centred[:, :, :], per_token(rstd[:, :]), ALU.mult)\
                            .then_inc(xn_ready, 1)
                        set_up()
                    if s == DVE_AT["ctx3"] and T:
                        norm_ctx(b - 1, 3, b, inner)
                    if s == ACT_AT["k"] and not inner and b == -1:
                        wait_emptied(dve, b, "k", inner)
                        split_qk(dve, b, 1)
                    if s == DVE_AT["v"] and F:
                        wait_filled(dve, b, "v", inner)
                        V.scalar_tensor_tensor(
                            out=v_ones[1 - par][:, :, :, 0:HD].rearrange("p t h d -> p (t h) d"),
                            in0=desk_bank[DESK["v"]][:, :].rearrange("p (a d) -> p a d", d=HD),
                            scalar=scales[:, 2:3], in1=b_v_all.rearrange("p (a d) -> p a d", d=HD),
                            op0=ALU.mult, op1=ALU.add).then_inc(emptied[DESK["v"]], 1)
                    if s == DVE_AT["proj"] and T:
                        wait_filled(dve, b, "proj", inner)
                        wait(dve, xb_ready, b)
                        wait(dve, mixed, 1 + 16 * (b - 1))
                        V.scalar_tensor_tensor(
                            out=x1[:, :, :].rearrange("p t d -> p (t d)"), in0=desk_bank[DESK["proj"]][:, :],
                            scalar=scales[:, 3:4], in1=x_bias[:, :, :].rearrange("p t d -> p (t d)"),
                            op0=ALU.mult, op1=ALU.add).then_inc(emptied[DESK["proj"]], 1)
                    if s == DVE_AT["stats2"] and T:
                        wait_emptied(dve, b, "proj", inner)
                        for t in range(QT):
                            last = V.bn_stats(stats2[:, t, :], x1[:, t, :])
                        last.then_inc(ln2, 1)
                    if s == DVE_AT["aggr2"] and T:
                        for t in range(QT):
                            last = V.bn_aggr(mean_var2[:, t, :], stats2[:, t, :])
                        last.then_inc(ln2, 1)
                    if s == DVE_AT["var2"] and T:
                        wait(dve, ln2, 3 * (b - 1) + 2)
                        V.tensor_scalar(var_eps2[:, :], mean_var2[:, :, 1], EPS, None, ALU.add).then_inc(ln2, 1)
                    if s == DVE_AT["var2"] and is_last(b, inner):
                        V.tensor_tensor(x1_centred[:, :, :], x1[:, :, :], per_token(mean_var2[:, :, 0]),
                                        ALU.subtract).then_inc(dve_centred, 1)
                        dve.wait_ge(dve_centred, 2)
                        dve.wait_ge(ln2_centred, 2 * B)
                        V.tensor_tensor(xn2[:, :, :], x1_centred[:, :, :], per_token(rstd2[:, :]), ALU.mult)\
                            .then_inc(xn2_ready, 1)
                    if s == DVE_AT["ctx0"] and A:
                        norm_ctx(b, 0, b, inner)
                    if s == DVE_AT["logits"] and T:
                        wait_filled(dve, b, "logits", inner)
                        V.tensor_tensor(logits[:, :, :],
                                        desk_bank[DESK["logits"]][:, 0:QT * TOPW].rearrange("p (t e) -> p t e", e=TOPW),
                                        gate_b_all.unsqueeze(1).to_broadcast([P, QT, TOPW]),
                                        ALU.add).then_inc(emptied[DESK["logits"]], 1)
                    if s == DVE_AT["gate1"] and T:
                        wait_emptied(dve, b, "logits", inner)
                        step(1, V.reduce_max(g4[:, 0, :], logits[:, :, :], AX_X, negate=True))
                        after(1)
                        step(2, V.tensor_tensor(g10[:, 0, :, :], logits[:, :, :], wide(g4[:, 0, :]), ALU.add))
                    if s == DVE_AT["gate3"] and T:
                        wait(dve, gate_exp, b)
                        step(3, V.reduce_sum(g4[:, 1, :], g10[:, 1, :, :], AX_X))
                        after(3)
                        step(4, V.reciprocal(g4[:, 2, :], g4[:, 1, :]))
                    if s == DVE_AT["gate5"] and T:
                        after(4)
                        step(5, V.tensor_tensor(g10[:, 2, :, :], g10[:, 1, :, :], wide(g4[:, 2, :]), ALU.mult))
                        after(5)
                        step(6, V.reduce_max(g4[:, 3, :], g10[:, 2, :, :], AX_X))
                    if s == DVE_AT["gate7"] and T:
                        after(6)
                        step(7, V.tensor_tensor(g10[:, 3, :, :], g10[:, 2, :, :], wide(g4[:, 3, :]), ALU.subtract))
                        after(7)
                        step(8, V.scalar_tensor_tensor(out=g10[:, 4, :, :], in0=g10[:, 3, :, :], scalar=0.0,
                                                       in1=order[:, :, :], op0=ALU.is_ge, op1=ALU.mult))
                    if s == DVE_AT["gate9"] and T:
                        after(8)
                        step(9, V.reduce_max(g4[:, 4, :], g10[:, 4, :, :], AX_X))
                        after(9)
                        step(10, V.tensor_tensor(g10[:, 5, :, :], g10[:, 4, :, :], wide(g4[:, 4, :]), ALU.is_equal))
                    if s == DVE_AT["gate11"] and T:
                        after(10)
                        step(11, V.scalar_tensor_tensor(out=g10[:, 6, :, :], in0=g10[:, 5, :, :], scalar=-2.0,
                                                        in1=g10[:, 2, :, :], op0=ALU.mult, op1=ALU.add))
                        after(11)
                        step(12, V.reduce_max(g4[:, 5, :], g10[:, 6, :, :], AX_X))
                    if s == DVE_AT["ctx1"] and A:
                        norm_ctx(b, 1, b, inner)
                    if s == DVE_AT["gate13"] and T:
                        after(12)
                        step(13, V.tensor_tensor(g10[:, 7, :, :], g10[:, 6, :, :], wide(g4[:, 5, :]), ALU.subtract))
                        after(13)
                        step(14, V.scalar_tensor_tensor(out=g10[:, 8, :, :], in0=g10[:, 7, :, :], scalar=0.0,
                                                        in1=order[:, :, :], op0=ALU.is_ge, op1=ALU.mult))
                    if s == DVE_AT["gate15"] and T:
                        after(14)
                        step(15, V.reduce_max(g4[:, 6, :], g10[:, 8, :, :], AX_X))
                        after(15)
                        step(16, V.tensor_tensor(g10[:, 9, :, :], g10[:, 8, :, :], wide(g4[:, 6, :]), ALU.is_equal))
                        after(16)
                        step(17, V.tensor_tensor(chosen[:, :, :], g10[:, 5, :, 0:NE], g10[:, 9, :, 0:NE], ALU.add))
                    if s == DVE_AT["gate18"] and T:
                        after(17)
                        step(18, V.tensor_tensor(true_w[:, :, :], g10[:, 2, :, 0:NE], chosen[:, :, :], ALU.mult))
                        after(18)
                        step(19, V.reduce_sum(g4[:, 7, :], true_w[:, :, :], AX_X))
                        after(19)
                        step(20, V.scalar_tensor_tensor(out=g4[:, 8, :], in0=g4[:, 7, :], scalar=0.0,
                                                        in1=g4[:, 7, :], op0=ALU.is_le, op1=ALU.add))
                    if s == DVE_AT["gate21"] and T:
                        after(20)
                        step(21, V.reciprocal(g4[:, 9, :], g4[:, 8, :]))
                        after(21)
                        step(22, V.tensor_tensor(combine_w[:, :, :], true_w[:, :, :],
                                                 g4[:, 9, :].unsqueeze(2).to_broadcast([P, QT, NE]), ALU.mult))
                    if s == DVE_AT["gate21"] and T:
                        after(22)
                    for name in WEIGH:
                        if s == DVE_AT.get(name) and T and not is_last(b, inner):
                            weigh_here(b, name, inner)
                    if s == DVE_AT["ctx2"] and A:
                        norm_ctx(b, 2, b, inner)
                if is_last(b, inner):
                    for name in WEIGH:
                        weigh_here(b, name, inner)
                        t = int(name[1])
                        if name[2] == "b" and t % 2:
                            wait_emptied(dve, b, name, inner)
                            if t == 1:
                                dve.wait_ge(y_free, 16 * B)
                            mix(dve, t, (last_sum4, last_sum2, last_sum1), last_mixed, 2 * (t - 1))

            clear_k(nc.vector, 0, 0)
            dve.wait_ge(x0_loaded, 16)
            bodies(dve, body)

        @block.tensor
        def _(pe):
            T_ = nc.tensor
            def keep_warm(moving, n):
                for _ in range(n):
                    T_.matmul(st_bank[0][:, 0:moving.shape[-1]], identity_bf[:, :], moving, start=True, stop=True)

            pe.wait_ge(pool_setup, POOL_SETUP)
            keep_warm(identity_bf[:, :], WARM_FIRST)
            pe.wait_ge(w_loaded, W_DMAS * 16)

            def scores_t(b, s, par):
                g, t, c = s // 16, s % 16 // 4, s % 4
                if s % 16 == 0:
                    wait(pe, rows_max, 16 * (4 * b + g + 1))
                wait(pe, exp_done, SLOTS * b + s - 1)
                T_.matmul(st_bank[s % 2][:, :], k_rows[par][:, 4 * g + c, P * t:P * t + P], q_rows[par][:, 4 * g + c, :],
                          start=True, stop=True).then_inc(st_filled, 1)

            def scores(b, s, par):
                u = SLOTS * b + s + LEAD
                g, t, c = (s + LEAD) % SLOTS // 16, (s + LEAD) % 16 // 4, (s + LEAD) % 4
                if s == SLOTS - LEAD:
                    wait(pe, rows_qk, 16 * LOADS * (b + 2))
                wait(pe, max_done, u - 1 if s in (1, SLOTS - 1) else u - 2)
                T_.matmul(s_bank[s_bank_of(s)][:, :], q_rows[par][0:ROW_MAX, 4 * g + c, P * t:P * t + P],
                          k_rows[par][0:ROW_MAX, 4 * g + c, :],
                          start=True, stop=True).then_inc(s_filled, 1)

            def values(b, n, par):
                g, t = n // 4, n % 4
                wait(pe, exp_done, SLOTS * b + 4 * n + 4)
                if t == 0:
                    wait(pe, pv_taken, 4 * b + g)
                for c in range(4):
                    last = T_.matmul(pv_bank[32 * c:32 * c + 32, :], v_ones[par][:, t, 4 * g + c, :],
                                     probs[:, 4 * (n % 2) + c, :], start=t == 0, stop=t == QT - 1)
                last.then_inc(pv_done, 1)

            def task(b, name, par, inner):
                desk, bank = DESK[name], desk_bank[DESK[name]]
                if name in WEIGH and is_last(b, inner):
                    bank = last_bank[name]
                    if bank in desk_bank:
                        wait_emptied(pe, b, "logits", inner)
                else:
                    wait(pe, emptied[desk], place(b, name, inner))
                if name.startswith("rows"):
                    g = int(name[-1])
                    n = 4 * (b + (g == 0)) + g
                    wait(pe, max_split, 4 * n + 4)
                    rows = bank[0:12, 0:S // 2].bitcast(BF16)
                    for t in range(QT):
                        last = T_.transpose(rows[:, P * t:P * t + P], max_parts[:, g % 2, t, :], identity_bf[:, :])
                elif name == "xn_t":
                    wait(pe, xn_ready, b + 2)
                    for t in range(QT):
                        last = T_.transpose(bank[:, P * t:P * t + P], xn[:, t, :], identity[:, :])
                elif name in "qk":
                    wait_emptied(pe, b, "xn_t", inner)
                    last = T_.matmul(bank[:, :], w_qk_t[:, "qk".index(name), :], xn_t[:, :], start=True, stop=True)
                elif name == "v":
                    for t in range(QT):
                        last = T_.matmul(bank[:, P * t:P * t + P], xn_t[:, P * t:P * t + P], w_v_t,
                                         start=True, stop=True)
                elif name in ("ctx0", "ctx1", "ctx2", "ctx3"):
                    g = int(name[-1])
                    wait(pe, pv_taken, 4 * (b - (g == 3)) + g + 1)
                    for t in range(QT):
                        last = T_.transpose(bank[:, P * t:P * t + P], ctx_raw[:, g % 2, P * t:P * t + P],
                                            identity[:, :])
                elif name == "ctx_t":
                    wait_emptied(pe, b, "ctx3", inner)
                    for t in range(QT):
                        last = T_.transpose(bank[:, P * t:P * t + P], ctx_tok[:, t, :], identity[:, :])
                elif name == "proj":
                    wait_emptied(pe, b, "ctx_t", inner)
                    for t in range(QT):
                        last = T_.matmul(bank[:, P * t:P * t + P], ctx_t[:, P * t:P * t + P], w_o_t,
                                         start=True, stop=True)
                elif name == "xn2_t":
                    wait(pe, xn2_ready, b)
                    for t in range(QT):
                        last = T_.transpose(bank[:, P * t:P * t + P], xn2[:, t, :], identity[:, :])
                elif name == "logits":
                    wait_emptied(pe, b, "xn2_t", inner)
                    for t in range(QT):
                        last = T_.matmul(bank[:, TOPW * t:TOPW * t + TOPW], xn2_t[:, P * t:P * t + P], gate_t,
                                         start=True, stop=True)
                else:
                    t, half = int(name[1]), "ab".index(name[2])
                    T_.matmul(bank[:, :], xn2_t[:, P * t:P * t + P],
                              w_exp[:, 512 * half:512 * half + 512], start=True, stop=False)
                    last = T_.matmul(bank[:, :], ones3[:, :], eb_rows[:, 512 * half:512 * half + 512],
                                     start=False, stop=True)
                last.then_inc(filled[desk], 1)

            def body(b, par, inner):
                here = dict(zip("AFT", parts_of(b, inner)))
                if not inner and b == 0:
                    pe.wait_ge(v_ones_set, 1)
                for s in range(SLOTS):
                    if here["A"]:
                        scores_t(b, s, par)
                    for own_b, own_s in scores_in(b, s, inner):
                        if own_s < SLOTS - LEAD and here["A"]:
                            scores(own_b, own_s, par)
                        if own_s >= SLOTS - LEAD and here["F"]:
                            scores(own_b, own_s, par if not inner and own_b < b else 1 - par)
                    if s % 4 == PV_PHASE:
                        if s > 3 and here["A"]:
                            values(b, s // 4 - 1, par)
                        if s < 4 and here["T"]:
                            values(b - 1, 15, 1 - par)
                    if s in PE_SLOT and here[WHO[PE_SLOT[s]]]:
                        task(b, PE_SLOT[s], par, inner)
                        if PE_SLOT[s] == "proj" and is_last(b, inner):
                            keep_warm(q_rows[1][:, 0, :], WARM_LAST)
                if not inner and b == 0:
                    pe.wait_ge(eb_loaded, 16)

            bodies(pe, body)


def kernel(**inputs):
    import concourse.bacc as _bacc
    from concourse.bass_utils import run_bass_kernel_spmd as _run

    a = {name[3:]: np.asarray(v) for name, v in inputs.items()}
    qk_order = np.arange(P).reshape(HEADS, HD).T.ravel()
    weights = np.concatenate([a["attn_w_q"].T[:, qk_order], a["attn_w_k"].T[:, qk_order], a["attn_w_v"].T,
                              a["attn_w_o"].T, a["ffn_gate_w"].T], axis=1)
    scalars = [a[f"attn_s_{n}"].reshape(1) for n in "qkvo"]
    arrays = {
        "x": a["attn_x"],
        "weights": weights,
        "experts": a["ffn_expert_w"].transpose(1, 0, 2).reshape(P, NE * P),
        "vectors": np.concatenate([np.tile(a["attn_b_v"], 4), a["attn_b_o"], a["ffn_gate_b"]] + scalars),
        "qk_biases": np.stack([a["attn_b_q"][qk_order], a["attn_b_k"][qk_order]], axis=1),
        "expert_b": a["ffn_expert_b"],
    }
    arrays = {name: np.ascontiguousarray(v) for name, v in arrays.items()}
    nc = _bacc.Bacc("TRN2", target_bir_lowering=False, num_devices=1)
    args = [nc.dram_tensor(name, v.shape, mybir.dt.from_np(v.dtype), kind="ExternalInput").ap()
            for name, v in arrays.items()]
    args.append(nc.dram_tensor("layer_out", arrays["x"].shape, F32, kind="ExternalOutput").ap())
    build(nc, *args)
    return _run(nc, [arrays], core_ids=[0]).results[0]["layer_out"]
```
